# Optimizing a Trainium2 kernel written in Bass

```python
import numpy as np
import jax
import jax.numpy as jnp

def _softmax(x, axis=-1):
    return jax.nn.softmax(x, axis=axis)

def _gelu(x):
    return jax.nn.gelu(x, approximate=True)

def _silu(x):
    return jax.nn.silu(x)

def _sigmoid(x):
    return jax.nn.sigmoid(x)

def _layernorm(x, axis=-1, eps=1e-05):
    m = jnp.mean(x, axis=axis, keepdims=True)
    v = jnp.var(x, axis=axis, keepdims=True)
    return (x - m) / jnp.sqrt(v + eps)

def _scatter_add(tgt, idx, src, axis=0):
    return tgt.at[idx].add(src)

def _segment_sum(src, seg, n):
    return jax.ops.segment_sum(src, seg, n)
kernel_name = 'mk_flamingo_gated_d1_seqx_r2_308a24'

def setup_inputs(seed: int=0):
    np.random.seed(seed)
    _w = jnp.asarray

    def _rec_inputs():
        import jax
        import jax.numpy as jnp
        _rk = jax.random.key(seed)
        x = 7.22e-05 + 1 * jax.random.normal(jax.random.fold_in(_rk, 1), (4, 1024, 512), jnp.float32)
        _lenS = 1024 - jax.random.randint(jax.random.fold_in(_rk, 7), (4,), 0, max(1, 1024 // 4) + 1, jnp.int32)
        _lenS2 = 2048 - jax.random.randint(jax.random.fold_in(_rk, 8), (4,), 0, max(1, 2048 // 4) + 1, jnp.int32)
        _ctx_768P = jax.random.normal(jax.random.fold_in(_rk, 11), (4, 16, 384), jnp.float32)
        _ctx_768c = jax.random.dirichlet(jax.random.fold_in(_rk, 511), 0.3 * jnp.ones((16,), jnp.float32), (4, 2048))
        _ctx_768t = jnp.einsum('bsk,bkd->bsd', _ctx_768c, _ctx_768P)
        _ctx_768t = _ctx_768t * jax.lax.rsqrt(jnp.mean(jnp.square(_ctx_768t)) + 1e-12) * 0.953939
        ctx_768 = -0.000191848 + 0.999787 * (_ctx_768t + 0.3 * jax.random.normal(jax.random.fold_in(_rk, 611), (4, 2048, 384), jnp.float32))
        _g = jax.random.normal(jax.random.fold_in(_rk, 9001), (2, 1), jnp.float32)
        _g = jnp.sign(_g) * jnp.maximum(jnp.abs(_g), 1.0) + (_g == 0) * 1.0
        g_xattn = _g[0]
        g_ffn = _g[1]
        return (x, ctx_768, g_xattn, g_ffn)
    x, ctx_768, g_xattn, g_ffn = _rec_inputs()

    def _L0_xattn_setup():
        import jax, jax.numpy as jnp
        import numpy as np
        NUM_HEADS = 16
        CLAMP = 10000.0
        key = jax.random.key(seed)
        ks = jax.random.split(key, 8)
        B, Nq, Nkv, Cq, Ckv = (4, 1024, 1024, 512, 384)
        s_q = 1.0 / np.sqrt(Cq)
        s_kv = 1.0 / np.sqrt(Ckv)
        return {'query': jax.random.normal(ks[0], (B, Nq, Cq), jnp.float32), 'key_value': jax.random.normal(ks[1], (B, Nkv, Ckv), jnp.float32), 'Wq': jax.random.normal(ks[2], (Cq, Cq), jnp.float32) * s_q, 'bq': jnp.zeros((Cq,), jnp.float32), 'Wk': jax.random.normal(ks[3], (Ckv, Cq), jnp.float32) * s_kv, 'bk': jnp.zeros((Cq,), jnp.float32), 'Wv': jax.random.normal(ks[4], (Ckv, Cq), jnp.float32) * s_kv, 'bv': jnp.zeros((Cq,), jnp.float32), 'Wo': jax.random.normal(ks[5], (Cq, Cq), jnp.float32) * s_q, 'bo': jnp.zeros((Cq,), jnp.float32)}
    _L0_xattn_all = _L0_xattn_setup()
    _L0_xattn_in = {k: v for k, v in _L0_xattn_all.items() if k in ('Wq', 'bq', 'Wk', 'bk', 'Wv', 'bv', 'Wo', 'bo')}
    del _L0_xattn_all

    def _L0_ffn_setup():
        import jax, jax.numpy as jnp
        import numpy as np
        B, S, H, F, G = (8, 1024, 512, 2048, 128)
        EPS = 1e-05

        def _dequant(q, scales, g):
            K, N = q.shape
            w = (q.astype(jnp.float32) - 128.0).reshape(K // g, g, N) * scales[:, None, :]
            return w.reshape(K, N)
        key = jax.random.key(seed)
        ks = jax.random.split(key, 8)
        x = jax.random.normal(ks[0], (B, S, H), dtype=jnp.float32)
        ln_gamma = jnp.ones((H,), jnp.float32)
        ln_beta = jnp.zeros((H,), jnp.float32)
        fc1_q = jax.random.randint(ks[1], (H, F), 0, 128, dtype=jnp.int32)
        fc2_q = jax.random.randint(ks[2], (F, H), 0, 128, dtype=jnp.int32)
        fc1_scales = jax.random.uniform(ks[3], (H // G, F), jnp.float32) * 0.02 + 0.001
        fc2_scales = jax.random.uniform(ks[4], (F // G, H), jnp.float32) * 0.02 + 0.001
        fc1_bias = jax.random.normal(ks[5], (F,), jnp.float32) * 0.02
        fc2_bias = jax.random.normal(ks[6], (H,), jnp.float32) * 0.02
        return {'x': x, 'ln_gamma': ln_gamma, 'ln_beta': ln_beta, 'fc1_q': fc1_q, 'fc1_scales': fc1_scales, 'fc1_bias': fc1_bias, 'fc2_q': fc2_q, 'fc2_scales': fc2_scales, 'fc2_bias': fc2_bias}
    _L0_ffn_all = _L0_ffn_setup()
    _L0_ffn_in = {k: v for k, v in _L0_ffn_all.items() if k in ('ln_gamma', 'ln_beta', 'fc1_q', 'fc1_scales', 'fc1_bias', 'fc2_q', 'fc2_scales', 'fc2_bias')}
    del _L0_ffn_all
    return {'x': x, 'ctx_768': ctx_768, 'g_xattn': g_xattn, 'g_ffn': g_ffn, 'L0_xattn_Wq': _L0_xattn_in['Wq'], 'L0_xattn_bq': _L0_xattn_in['bq'], 'L0_xattn_Wk': _L0_xattn_in['Wk'], 'L0_xattn_bk': _L0_xattn_in['bk'], 'L0_xattn_Wv': _L0_xattn_in['Wv'], 'L0_xattn_bv': _L0_xattn_in['bv'], 'L0_xattn_Wo': _L0_xattn_in['Wo'], 'L0_xattn_bo': _L0_xattn_in['bo'], 'L0_ffn_ln_gamma': _L0_ffn_in['ln_gamma'], 'L0_ffn_ln_beta': _L0_ffn_in['ln_beta'], 'L0_ffn_fc1_q': _L0_ffn_in['fc1_q'], 'L0_ffn_fc1_scales': _L0_ffn_in['fc1_scales'], 'L0_ffn_fc1_bias': _L0_ffn_in['fc1_bias'], 'L0_ffn_fc2_q': _L0_ffn_in['fc2_q'], 'L0_ffn_fc2_scales': _L0_ffn_in['fc2_scales'], 'L0_ffn_fc2_bias': _L0_ffn_in['fc2_bias']}

def reference(x, ctx_768, g_xattn, g_ffn, L0_xattn_Wq, L0_xattn_bq, L0_xattn_Wk, L0_xattn_bk, L0_xattn_Wv, L0_xattn_bv, L0_xattn_Wo, L0_xattn_bo, L0_ffn_ln_gamma, L0_ffn_ln_beta, L0_ffn_fc1_q, L0_ffn_fc1_scales, L0_ffn_fc1_bias, L0_ffn_fc2_q, L0_ffn_fc2_scales, L0_ffn_fc2_bias):
    import jax
    import jax.numpy as jnp

    def _L0_xattn_ref(query, key_value, Wq, bq, Wk, bk, Wv, bv, Wo, bo):
        import jax, jax.numpy as jnp
        import numpy as np
        NUM_HEADS = 16
        CLAMP = 10000.0
        B, Nq, Cq = query.shape
        Nkv = key_value.shape[1]
        H = NUM_HEADS
        D = Cq // H
        scale = D ** (-0.5)
        q = (query @ Wq + bq).reshape(B, Nq, H, D).transpose(0, 2, 1, 3)
        k = (key_value @ Wk + bk).reshape(B, Nkv, H, D).transpose(0, 2, 1, 3)
        v = (key_value @ Wv + bv).reshape(B, Nkv, H, D).transpose(0, 2, 1, 3)
        attn = jnp.einsum('bhqd,bhkd->bhqk', q, k) * scale
        attn = jnp.clip(attn, -CLAMP, CLAMP)
        attn = jax.nn.softmax(attn, axis=-1)
        attn = jnp.where(jnp.any(jnp.isnan(attn)), jnp.asarray(1.0 / Nkv, attn.dtype), attn)
        x = jnp.einsum('bhqk,bhkd->bqhd', attn, v).reshape(B, Nq, Cq)
        return x @ Wo + bo

    def _L0_ffn_ref(x, ln_gamma, ln_beta, fc1_q, fc1_scales, fc1_bias, fc2_q, fc2_scales, fc2_bias):
        import jax, jax.numpy as jnp
        import numpy as np
        B, S, H, F, G = (8, 1024, 512, 2048, 128)
        EPS = 1e-05

        def _dequant(q, scales, g):
            K, N = q.shape
            w = (q.astype(jnp.float32) - 128.0).reshape(K // g, g, N) * scales[:, None, :]
            return w.reshape(K, N)
        residual = x
        mu = jnp.mean(x, axis=-1, keepdims=True)
        var = jnp.mean(jnp.square(x - mu), axis=-1, keepdims=True)
        h = (x - mu) * jax.lax.rsqrt(var + EPS) * ln_gamma + ln_beta
        hf = h.reshape(-1, H)
        w1 = _dequant(fc1_q, fc1_scales, G)
        y = hf @ w1 + fc1_bias
        y = jax.nn.silu(y)
        w2 = _dequant(fc2_q, fc2_scales, G)
        z = y @ w2 + fc2_bias
        return residual + 0.5 * z.reshape(residual.shape)
    x = x + jnp.tanh(g_xattn[0]) * _L0_xattn_ref(_layernorm(x, axis=-1), ctx_768, L0_xattn_Wq, L0_xattn_bq, L0_xattn_Wk, L0_xattn_bk, L0_xattn_Wv, L0_xattn_bv, L0_xattn_Wo, L0_xattn_bo)
    x = x + jnp.tanh(g_ffn[0]) * _L0_ffn_ref(_layernorm(x, axis=-1), L0_ffn_ln_gamma, L0_ffn_ln_beta, L0_ffn_fc1_q, L0_ffn_fc1_scales, L0_ffn_fc1_bias, L0_ffn_fc2_q, L0_ffn_fc2_scales, L0_ffn_fc2_bias)
    return x

_drawn_inputs = setup_inputs


def setup_inputs(seed=0):
    import zlib

    import numpy as np

    out = dict(_drawn_inputs(seed))
    spreads = {'L0_xattn_bq': (0.0, 0.8),
     'L0_xattn_bk': (0.0, 0.8),
     'L0_xattn_bv': (0.0, 0.457),
     'L0_xattn_bo': (0.0, 0.603),
     'L0_ffn_ln_gamma': (1.0, 0.2),
     'L0_ffn_ln_beta': (0.0, 0.1)}
    factors = {'L0_ffn_fc1_bias': 8.0, 'L0_ffn_fc2_bias': 8.0}
    for name, (base, spread) in spreads.items():
        noise = np.random.default_rng([zlib.crc32(name.encode()), seed]).standard_normal(out[name].shape)
        drawn = base * np.exp(spread * noise) if base else spread * noise
        out[name] = jnp.asarray(drawn.astype(out[name].dtype))
    for name, factor in factors.items():
        out[name] = (out[name] * factor).astype(out[name].dtype)
    return out
```

```python
from contextlib import ExitStack

import concourse.bass as bass
from concourse import mybir

ALU = mybir.AluOpType
ACT = mybir.ActivationFunctionType
AX_X = mybir.AxisListType.X
F32 = mybir.dt.float32
F32R = mybir.dt.float32r
I32 = mybir.dt.int32

P = 128
BANK = 512
HEADS = 16
D = 32
CLAMP = 10000.0
EPS = 1e-5
ZERO_POINT = 128.0



def need(eng, sem, value):
    if isinstance(value, int) and value <= 0:
        return
    eng.wait_ge(sem, value)


def wait_alone(eng, sem, value, passed):
    eng.wait_ge(sem, value)
    eng.sem_inc(passed, 1)


def at(base, slot, lag, unroll, total):
    item = unroll * base + (slot - lag)
    if isinstance(item, int) and not 0 <= item < total:
        return None
    return item


def run_steps(eng, step, total, unroll, first=1, last=0, tail=0):
    bodies = total // unroll
    for base in range(first):
        for slot in range(unroll):
            step(base, slot)
    with eng.Fori(first, bodies - last) as base:
        for slot in range(unroll):
            step(base, slot)
    for s in range((bodies - last) * unroll, total + tail):
        step(s // unroll, s % unroll)


class Core:

    def __init__(self, nc, ctx):
        self.nc, self.ctx = nc, ctx
        self.ps = ctx.enter_context(nc.psum_tensor("ps", [P, 8, BANK], F32))

    def sb(self, ctx, name, shape, dt=F32):
        return ctx.enter_context(self.nc.sbuf_tensor(name, shape, dt))

    def sem(self, ctx, name):
        return ctx.enter_context(self.nc.semaphore(name))


def add_squares(pool, part, square, total, tiles, c, part_done, bound_done):
    for m in range(tiles):
        pool.wait_ge(part_done, tiles * c + m + 1)
        tile = part[:, m, :].bitcast(F32)
        need(pool, bound_done, 2 * (tiles * c + m))
        pool.tensor_tensor(square[:, :], tile, tile, ALU.mult).then_inc(bound_done, 1)
        pool.wait_ge(bound_done, 2 * (tiles * c + m) + 1)
        pool.tensor_tensor(total[:, :], total[:, :], square[:, :], ALU.add).then_inc(bound_done, 1)


def project_queries(k, A, x, wq, bq, qT_d):
    nc, ps = k.nc, k.ps
    B, SQ, C = x.shape
    KT = C // P
    CH = B * SQ // BANK
    PER = SQ // BANK
    TT = BANK // P
    SCALE = float(D) ** -0.5
    x_rows = x.rearrange("b (t p) c -> (b t) p c", p=P)

    with ExitStack() as ctx:
        sb = lambda name, shape, dt=F32: k.sb(ctx, "pq_" + name, shape, dt)
        sem = lambda name: k.sem(ctx, "pq_" + name)
        w = sb("w", [P, KT, C])
        w_hi = sb("w_hi", [P, KT, C], F32R)
        w_lo = sb("w_lo", [P, KT, C], F32R)
        bias_raw = sb("bias_raw", [P, KT])
        bias = sb("bias", [P, KT])
        eps = sb("eps", [P, 1])
        x_in = [sb(f"x_in{i}", [P, TT, C]) for i in range(2)]
        stats = sb("stats", [P, TT, 6])
        meanvar = sb("meanvar", [P, TT, 2])
        std = sb("std", [P, TT])
        rstd = sb("rstd", [P, TT])
        xT_hi = [sb(f"xT_hi{i}", [P, KT, BANK], F32R) for i in range(2)]
        xT_lo = [sb(f"xT_lo{i}", [P, KT, BANK], F32R) for i in range(2)]
        q_hi = [sb(f"q_hi{i}", [P, KT, BANK], F32R) for i in range(2)]
        q_lo = [sb(f"q_lo{i}", [P, KT, BANK], F32R) for i in range(2)]

        square = sb("square", [P, BANK])

        w_in = sem("w_in")
        setup = sem("setup")
        passed = sem("passed")
        const = sem("const")
        x_loaded = [sem(f"x_loaded{i}") for i in range(2)]
        stat_done = sem("stat_done")
        mv_done = sem("mv_done")
        std_done = sem("std_done")
        rstd_done = sem("rstd_done")
        norm_done = sem("norm_done")
        x_turned = sem("x_turned")
        xhi_done = sem("xhi_done")
        xlo_done = sem("xlo_done")
        q_done = sem("q_done")
        qhi_done = sem("qhi_done")
        qlo_done = sem("qlo_done")
        bound_done = sem("bound_done")
        finite_done = sem("finite_done")
        q_stored = [sem(f"q_stored{i}") for i in range(2)]
        block = ctx.enter_context(nc.Block())

        @block.gpsimd
        def _(pool):
            pool.memset(A["ident"][:, :], 0.0).then_inc(const, 1)
            pool.memset(A["fold"][:, :], 0.0).then_inc(const, 1)
            pool.memset(A["q_sq_sum"][:, :], 0.0).then_inc(const, 1)
            pool.memset(A["k_sq_sum"][:, :], 0.0).then_inc(const, 1)
            pool.memset(A["not_finite"][:, :], 0.0).then_inc(const, 1)
            pool.memset(eps[:, :], EPS).then_inc(const, 1)
            pool.wait_ge(const, 6)
            pool.affine_select(out=A["ident"][:, :], in_=A["ident"][:, :], compare_op=ALU.not_equal, fill=1.0,
                               base=0, pattern=[[-1, P]], channel_multiplier=1).then_inc(const, 1)
            for g in range(P // D):
                pool.affine_select(out=A["fold"][:, :], in_=A["fold"][:, :], compare_op=ALU.not_equal, fill=1.0,
                                   base=-D * g, pattern=[[-1, D]], channel_multiplier=1).then_inc(const, 1)
                pool.wait_ge(const, 8 + g)

            def step(base, slot):
                if (c := at(base, slot, 2, 2, CH)) is not None:
                    add_squares(pool, q_hi[slot], square, A["q_sq_sum"], KT, c, qhi_done, bound_done)

            run_steps(pool, step, CH, 2, first=2, tail=2)

        @block.sync
        def _(sp):
            def step(base, slot):
                if (s := at(base, slot, 0, 2, CH)) is not None:
                    need(sp, x_turned, KT * (s - 1))
                    sp.dma_start(x_in[slot][:, :, :], x_rows[bass.ds(TT * s, TT)].rearrange("t p c -> p t c")) \
                        .then_inc(x_loaded[slot], 16)
                if (c := at(base, slot, 2, 2, CH)) is not None:
                    need(sp, qhi_done, KT * (c + 1))
                    need(sp, qlo_done, KT * (c + 1))
                    for part, q in ((0, q_hi), (1, q_lo)):
                        dst = qT_d[part][bass.ds(C * (base - 1), C), BANK * slot:BANK * (slot + 1)]
                        sp.dma_start(dst.rearrange("(m p) n -> p m n", p=P), q[slot][:, :, :].bitcast(F32)) \
                            .then_inc(q_stored[slot], 16)

            assert PER == 2
            sp.dma_start(w[:, :, :], wq.rearrange("(k p) n -> p k n", p=P)).then_inc(w_in, 16)
            sp.dma_start(bias_raw[:, :], bq.rearrange("(m p) -> p m", p=P),
                         allow_slow_non_contiguous=True).then_inc(w_in, 16)
            run_steps(sp, step, CH, 2, first=2, tail=2)
            for i in range(2):
                sp.wait_ge(q_stored[i], 32 * (CH // 2))

        @block.tensor
        def _(pe):
            def step(base, slot):
                par = (slot - 1) % 2
                if (c := at(base, slot, 1, 2, CH)) is not None:
                    need(pe, norm_done, TT * (c + 1))
                    for kt in range(KT):
                        need(pe, xlo_done, KT * (c - 1) + kt + 1)
                        for t in range(TT):
                            mm = pe.transpose(ps[:, kt, P * t:P * (t + 1)], x_in[par][:, t, P * kt:P * (kt + 1)],
                                              A["ident"][:, :])
                        mm.then_inc(x_turned, 1)
                if (c := at(base, slot, 2, 2, CH)) is not None:
                    need(pe, xhi_done, KT * (c + 1))
                    need(pe, xlo_done, KT * (c + 1))
                    for m in range(KT):
                        need(pe, qlo_done, KT * (c - 1) + m + 1)
                        parts = [(a, b, kt) for kt in range(KT)
                                 for a, b in ((w_hi, xT_hi), (w_lo, xT_hi), (w_hi, xT_lo))]
                        for n, (a, b, kt) in enumerate(parts):
                            mm = pe.matmul(ps[:, 4 + m, :], a[:, kt, P * m:P * (m + 1)], b[slot][:, kt, :],
                                           start=(n == 0), stop=(n == len(parts) - 1))
                        mm.then_inc(q_done, 1)

            pe.wait_ge(const, 11)
            pe.wait_ge(setup, 4)
            run_steps(pe, step, CH, 2, first=2, tail=2)

        @block.scalar
        def _(act):
            def step(base, slot):
                par = (slot - 1) % 2
                if (c := at(base, slot, 1, 2, CH)) is not None:
                    need(act, q_done, KT * (c - 1))
                    for kt in range(KT):
                        need(act, x_turned, KT * c + kt + 1)
                        act.activation(xT_hi[par][:, kt, :], ps[:, kt, :], ACT.Identity).then_inc(xhi_done, 1)
                if (s := at(base, slot, 0, 2, CH)) is not None:
                    need(act, mv_done, TT * (s + 1))
                    act.activation(std[:, :], meanvar[:, :, 1], ACT.Sqrt, bias=eps[:, 0:1]).then_inc(std_done, 1)
                if (c := at(base, slot, 2, 2, CH)) is not None:
                    need(act, q_stored[slot], 32 * base - 32)
                    need(act, bound_done, 2 * KT * (c - 1))
                    for m in range(KT):
                        need(act, q_done, KT * c + m + 1)
                        act.activation(q_hi[slot][:, m, :], ps[:, 4 + m, :], ACT.Identity, bias=bias[:, m:m + 1]) \
                            .then_inc(qhi_done, 1)

            act.wait_ge(const, 6)
            act.wait_ge(setup, 4)
            run_steps(act, step, CH, 2, first=2, tail=2)

        @block.vector
        def _(dve):
            def step(base, slot):
                par = (slot - 1) % 2
                if (c := at(base, slot, 1, 2, CH)) is not None:
                    need(dve, q_done, KT * (c - 1))
                    for kt in range(KT):
                        need(dve, xhi_done, KT * c + kt + 1)
                        dve.tensor_tensor(xT_lo[par][:, kt, :], ps[:, kt, :], xT_hi[par][:, kt, :].bitcast(F32),
                                          ALU.subtract).then_inc(xlo_done, 1)
                if (s := at(base, slot, 0, 2, CH)) is not None:
                    dve.wait_ge(x_loaded[slot], 16 * base + 16)
                    for t in range(TT):
                        dve.bn_stats(stats[:, t, :], x_in[slot][:, t, :]).then_inc(stat_done, 1)
                    need(dve, std_done, s)
                    for t in range(TT):
                        wait_alone(dve, stat_done, TT * s + t + 1, passed)
                        dve.bn_aggr(meanvar[:, t, :], stats[:, t, :]).then_inc(mv_done, 1)
                    dve.wait_ge(std_done, s + 1)
                    dve.reciprocal(rstd[:, :], std[:, :]).then_inc(rstd_done, 1)
                    dve.wait_ge(rstd_done, s + 1)
                    dve.wait_ge(mv_done, TT * s + TT)
                    for t in range(TT):
                        dve.tensor_scalar(x_in[slot][:, t, :], x_in[slot][:, t, :], meanvar[:, t, 0:1],
                                          rstd[:, t:t + 1], ALU.subtract, ALU.mult).then_inc(norm_done, 1)
                if (c := at(base, slot, 2, 2, CH)) is not None:
                    need(dve, q_stored[slot], 32 * base - 32)
                    for m in range(KT):
                        dve.wait_ge(qhi_done, KT * c + m + 1)
                        hi = q_hi[slot][:, m, :].bitcast(F32)
                        dve.scalar_tensor_tensor(q_lo[slot][:, m, :], ps[:, 4 + m, :], bias[:, m:m + 1], hi,
                                                 ALU.add, ALU.subtract).then_inc(qlo_done, 1)
                        need(dve, finite_done, KT * c + m)
                        dve.scalar_tensor_tensor(A["not_finite"][:, :], hi, 0.0, A["not_finite"][:, :], ALU.mult,
                                                 ALU.add).then_inc(finite_done, 1)

            dve.wait_ge(w_in, 32)
            dve.wait_ge(const, 6)
            dve.tensor_scalar(w[:, :, :], w[:, :, :], SCALE, None, ALU.mult).then_inc(setup, 1)
            dve.tensor_scalar(bias[:, :], bias_raw[:, :], SCALE, None, ALU.mult).then_inc(setup, 1)
            dve.wait_ge(setup, 2)
            dve.tensor_copy(w_hi[:, :, :], w[:, :, :]).then_inc(setup, 1)
            dve.wait_ge(setup, 3)
            dve.tensor_tensor(w_lo[:, :, :], w[:, :, :], w_hi[:, :, :].bitcast(F32), ALU.subtract).then_inc(setup, 1)
            run_steps(dve, step, CH, 2, first=2, tail=2)


def project_keys_values(k, A, ctx_in, wk, bk, wv, bv, kT_d, v_d):
    nc, ps = k.nc, k.ps
    B, SK, CK = ctx_in.shape
    C = wk.shape[1]
    KT, MT = CK // P, C // P
    CH = B * SK // BANK
    PER = SK // BANK
    TT = BANK // P
    OUT = MT + TT
    rows = ctx_in.rearrange("b (t p) c -> (b t) p c", p=P)

    with ExitStack() as ctx:
        sb = lambda name, shape, dt=F32: k.sb(ctx, "kv_" + name, shape, dt)
        sem = lambda name: k.sem(ctx, "kv_" + name)
        w = [sb(f"w{i}", [P, KT, C]) for i in range(2)]
        w_hi = [sb(f"w_hi{i}", [P, KT, C], F32R) for i in range(2)]
        w_lo = [sb(f"w_lo{i}", [P, KT, C], F32R) for i in range(2)]
        k_bias = sb("k_bias", [P, MT])
        v_bias = sb("v_bias", [P, C])
        c_in = [sb(f"c_in{i}", [P, TT, CK]) for i in range(2)]
        cT_hi = [sb(f"cT_hi{i}", [P, KT, BANK], F32R) for i in range(2)]
        cT_lo = [sb(f"cT_lo{i}", [P, KT, BANK], F32R) for i in range(2)]
        k_hi = [sb(f"k_hi{i}", [P, MT, BANK], F32R) for i in range(2)]
        k_lo = [sb(f"k_lo{i}", [P, MT, BANK], F32R) for i in range(2)]
        v_out = [sb(f"v_out{i}", [P, HEADS, TT * D]) for i in range(2)]
        ends = sb("ends", [P, 4])
        square = sb("square", [P, BANK])
        one_row = sb("one_row", [1, P])
        found = sb("found", [1, 4])
        pick = sb("pick", [1, 4])

        w_in = sem("w_in")
        setup = sem("setup")
        passed = sem("passed")
        c_loaded = [sem(f"c_loaded{i}") for i in range(2)]
        c_turned = sem("c_turned")
        chi_done = sem("chi_done")
        clo_done = sem("clo_done")
        kv_done = sem("kv_done")
        khi_done = sem("khi_done")
        klo_done = sem("klo_done")
        v_done = sem("v_done")
        bound_done = sem("bound_done")
        finite_done = sem("finite_done")
        stored = [sem(f"stored{i}") for i in range(2)]
        path = sem("path")
        path_pe = sem("path_pe")
        block = ctx.enter_context(nc.Block())

        @block.gpsimd
        def _(pool):
            def step(base, slot):
                if (c := at(base, slot, 1, 2, CH)) is not None:
                    add_squares(pool, k_hi[(slot - 1) % 2], square, A["k_sq_sum"], MT, c, khi_done,
                                        bound_done)

            run_steps(pool, step, CH, 2, first=2, tail=1)

        @block.sync
        def _(sp):
            def step(base, slot):
                par = slot % 2
                if (s := at(base, slot, 0, PER, CH)) is not None:
                    need(sp, c_turned, KT * (s - 1))
                    sp.dma_start(c_in[par][:, :, :], rows[bass.ds(TT * s, TT)].rearrange("t p c -> p t c")) \
                        .then_inc(c_loaded[par], 16)
                if (c := at(base, slot, 1, PER, CH)) is not None:
                    batch, chunk = base + (slot - 1) // PER, (slot - 1) % PER
                    par = chunk % 2
                    need(sp, khi_done, MT * (c + 1))
                    need(sp, klo_done, MT * (c + 1))
                    for part, kk in ((0, k_hi), (1, k_lo)):
                        dst = kT_d[part][bass.ds(C * batch, C), BANK * chunk:BANK * (chunk + 1)]
                        sp.dma_start(dst.rearrange("(m p) n -> p m n", p=P), kk[par][:, :, :].bitcast(F32)) \
                            .then_inc(stored[par], 16)
                    need(sp, v_done, TT * (c + 1))
                    dst = v_d[bass.ds(HEADS * batch, HEADS), :, TT * D * chunk:TT * D * (chunk + 1)]
                    sp.dma_start(dst.rearrange("h p n -> p h n"), v_out[par][:, :, :]).then_inc(stored[par], 16)

            for i, src in enumerate((wk, wv)):
                sp.dma_start(w[i][:, :, :], src.rearrange("(k p) n -> p k n", p=P)).then_inc(w_in, 16)
            sp.dma_start(k_bias[:, :], bk.rearrange("(m p) -> p m", p=P),
                         allow_slow_non_contiguous=True).then_inc(w_in, 16)
            sp.dma_start(v_bias[:, :], bv.partition_broadcast(P)).then_inc(w_in, 16)
            run_steps(sp, step, CH, PER, first=1, tail=1)
            for i in range(2):
                sp.wait_ge(stored[i], 48 * (CH // 2))

        @block.tensor
        def _(pe):
            def step(base, slot):
                if (s := at(base, slot, 0, 2, CH)) is not None:
                    pe.wait_ge(c_loaded[slot], 16 * base + 16)
                    for kt in range(KT):
                        need(pe, clo_done, KT * (s - 1) + kt + 1)
                        for t in range(TT):
                            mm = pe.transpose(ps[:, kt, P * t:P * (t + 1)], c_in[slot][:, t, P * kt:P * (kt + 1)],
                                              A["ident"][:, :])
                        mm.then_inc(c_turned, 1)
                if (c := at(base, slot, 1, 2, CH)) is not None:
                    par = (slot - 1) % 2
                    need(pe, chi_done, KT * (c + 1))
                    need(pe, clo_done, KT * (c + 1))
                    for m in range(MT):
                        need(pe, v_done, TT * (c - 1) + m + 1)
                        parts = [(a, b, kt) for kt in range(KT)
                                 for a, b in ((w_hi, cT_hi), (w_lo, cT_hi), (w_hi, cT_lo))]
                        for n, (a, b, kt) in enumerate(parts):
                            mm = pe.matmul(ps[:, 4 + m, :], a[0][:, kt, P * m:P * (m + 1)], b[par][:, kt, :],
                                           start=(n == 0), stop=(n == len(parts) - 1))
                        mm.then_inc(kv_done, 1)
                    for t in range(TT):
                        need(pe, klo_done, MT * c + t + 1)
                        parts = [(a, b, kt) for kt in range(KT)
                                 for a, b in ((cT_hi, w_hi), (cT_hi, w_lo), (cT_lo, w_hi))]
                        for n, (a, b, kt) in enumerate(parts):
                            mm = pe.matmul(ps[:, 4 + t, :], a[par][:, kt, P * t:P * (t + 1)], b[1][:, kt, :],
                                           start=(n == 0), stop=(n == len(parts) - 1))
                        mm.then_inc(kv_done, 1)

            pe.wait_ge(setup, 4)
            run_steps(pe, step, CH, 2, first=2, tail=1)
            pe.wait_ge(path, 5)
            for i in range(3):
                mm = pe.transpose(ps[0:1, 0, P * i:P * (i + 1)], ends[:, i:i + 1], A["ident"][:, :])
            mm.then_inc(path_pe, 1)
            pe.wait_ge(path, 10)
            pe.matmul(ps[:, 1, 0:1], one_row[:, :], pick[:, 2:3], start=True, stop=True).then_inc(path_pe, 1)

        @block.scalar
        def _(act):
            def step(base, slot):
                if (s := at(base, slot, 0, 2, CH)) is not None:
                    need(act, kv_done, OUT * (s - 1))
                    for kt in range(KT):
                        need(act, c_turned, KT * s + kt + 1)
                        act.activation(cT_hi[slot][:, kt, :], ps[:, kt, :], ACT.Identity).then_inc(chi_done, 1)
                if (c := at(base, slot, 1, 2, CH)) is not None:
                    par = (slot - 1) % 2
                    need(act, stored[par], 48 * (base + (slot - 1) // 2))
                    need(act, bound_done, 2 * MT * (c - 1))
                    for m in range(MT):
                        need(act, kv_done, OUT * c + m + 1)
                        act.activation(k_hi[par][:, m, :], ps[:, 4 + m, :], ACT.Identity, bias=k_bias[:, m:m + 1]) \
                            .then_inc(khi_done, 1)

            act.wait_ge(w_in, 64)
            run_steps(act, step, CH, 2, first=2, tail=1)

        @block.vector
        def _(dve):
            def step(base, slot):
                if (s := at(base, slot, 0, 2, CH)) is not None:
                    need(dve, kv_done, OUT * (s - 1))
                    for kt in range(KT):
                        need(dve, chi_done, KT * s + kt + 1)
                        dve.tensor_tensor(cT_lo[slot][:, kt, :], ps[:, kt, :], cT_hi[slot][:, kt, :].bitcast(F32),
                                          ALU.subtract).then_inc(clo_done, 1)
                if (c := at(base, slot, 1, 2, CH)) is not None:
                    par = (slot - 1) % 2
                    need(dve, stored[par], 48 * (base + (slot - 1) // 2))
                    for m in range(MT):
                        dve.wait_ge(khi_done, MT * c + m + 1)
                        hi = k_hi[par][:, m, :].bitcast(F32)
                        dve.scalar_tensor_tensor(k_lo[par][:, m, :], ps[:, 4 + m, :], k_bias[:, m:m + 1], hi,
                                                 ALU.add, ALU.subtract).then_inc(klo_done, 1)
                        need(dve, finite_done, MT * c + m)
                        dve.scalar_tensor_tensor(A["not_finite"][:, :], hi, 0.0, A["not_finite"][:, :], ALU.mult,
                                                 ALU.add).then_inc(finite_done, 1)
                    for t in range(TT):
                        dve.wait_ge(kv_done, OUT * c + MT + t + 1)
                        dve.tensor_tensor(v_out[par][:, :, D * t:D * (t + 1)],
                                          ps[:, 4 + t, :].rearrange("p (h d) -> p h d", d=D),
                                          v_bias[:, :].rearrange("p (h d) -> p h d", d=D), ALU.add) \
                            .then_inc(v_done, 1)

            dve.wait_ge(w_in, 64)
            for i in range(2):
                dve.tensor_copy(w_hi[i][:, :, :], w[i][:, :, :]).then_inc(setup, 1)
            for i in range(2):
                dve.wait_ge(setup, i + 1)
                dve.tensor_tensor(w_lo[i][:, :, :], w[i][:, :, :], w_hi[i][:, :, :].bitcast(F32),
                                  ALU.subtract).then_inc(setup, 1)
            run_steps(dve, step, CH, 2, first=2, tail=1)
            dve.wait_ge(finite_done, MT * CH)
            dve.wait_ge(bound_done, 2 * MT * CH)
            dve.tensor_reduce(ends[:, 0:1], A["q_sq_sum"][:, :], AX_X, ALU.max).then_inc(path, 1)
            dve.tensor_reduce(ends[:, 1:2], A["k_sq_sum"][:, :], AX_X, ALU.max).then_inc(path, 1)
            dve.tensor_reduce(ends[:, 3:4], A["not_finite"][:, :], AX_X, ALU.add).then_inc(path, 1)
            dve.memset(one_row[:, :], 1.0).then_inc(path, 1)
            dve.wait_ge(path, 4)
            dve.tensor_tensor(ends[:, 2:3], ends[:, 3:4], ends[:, 3:4], ALU.not_equal).then_inc(path, 1)
            dve.wait_ge(path_pe, 1)
            dve.tensor_reduce(found[:, 0:3], ps[0:1, 0, 0:3 * P].rearrange("p (i n) -> p i n", n=P), AX_X,
                              ALU.max).then_inc(path, 1)
            dve.wait_ge(path, 6)
            dve.tensor_tensor(pick[:, 0:1], found[:, 0:1], found[:, 1:2], ALU.mult).then_inc(path, 1)
            dve.wait_ge(path, 7)
            dve.tensor_scalar(pick[:, 1:2], pick[:, 0:1], (0.99 * CLAMP / D) ** 2, None, ALU.is_gt).then_inc(path, 1)
            dve.tensor_scalar(pick[:, 2:3], found[:, 2:3], -CLAMP, CLAMP, ALU.mult, ALU.add).then_inc(path, 1)
            dve.wait_ge(path, 9)
            dve.tensor_tensor(A["clip_path"][:, :], pick[:, 1:2], found[:, 2:3], ALU.max).then_inc(path, 1)
            dve.wait_ge(path_pe, 2)
            dve.tensor_copy(A["clip_high"][:, :], ps[:, 1, 0:1]).then_inc(path, 1)
            dve.wait_ge(path, 11)
            dve.tensor_scalar(A["clip_low"][:, :], A["clip_high"][:, :], -1.0, None, ALU.mult).then_inc(path, 1)


def attend(k, A, shape, qT_d, kT_d, v_d, o_d, w1_q, w1_s, w2_q, w2_s, w1_d, w2_d):
    nc, ps = k.nc, k.ps
    B, SQ, SK = shape
    N_HEADS = B * HEADS
    HALVES = SQ // BANK
    QT = BANK // P
    PER_HEAD = HALVES * QT
    UNROLL = 2 * PER_HEAD
    STEPS = N_HEADS * PER_HEAD
    KVT = SK // P
    GROUPS = KVT // 4
    SCORE, TURN, PV, PART, FOLD, NORM = 0, 2, 6, 10, 11, 12
    assert SK == 4 * BANK and HALVES == 2 and GROUPS == 4

    def on_act(t, g):
        return g < 2 or (g == 2 and t % 2 == 0)

    def copies(act, base, slot, g):
        of = [[sum(on_act(t, i) == act for i in range(n)) for n in range(GROUPS + 1)] for t in range(2)]
        pair = of[0][GROUPS] + of[1][GROUPS]
        n = pair * (slot // 2) + (of[0][GROUPS] if slot % 2 else 0) + of[slot % 2][g + 1]
        return pair * (UNROLL // 2) * base + n

    with ExitStack() as ctx:
        sb = lambda name, shape, dt=F32: k.sb(ctx, "at_" + name, shape, dt)
        sem = lambda name: k.sem(ctx, "at_" + name)
        k_stack = [sb(f"k_stack{i}", [P, SK], F32R) for i in range(2)]
        q_stack = [sb(f"q_stack{i}", [P, SQ], F32R) for i in range(2)]
        v_head = [sb(f"v_head{i}", [P, KVT, D]) for i in range(2)]
        score = [sb(f"score{i}", [P, SK]) for i in range(2)]
        prob = [sb(f"prob{i}", [P, SK]) for i in range(4)]
        probT = [sb(f"probT{i}", [P, KVT, BANK]) for i in range(2)]
        half_max = sb("half_max", [P, 2, 2])
        row_max = sb("row_max", [P, 2])
        neg_max = sb("neg_max", [P, 4])
        row_sum = sb("row_sum", [P, UNROLL])
        inv_sum = sb("inv_sum", [P, 2, QT])
        partial = sb("partial", [P, BANK])
        o_pair = sb("o_pair", [P, PER_HEAD, 2 * D])
        code = sb("code", [P, BANK], I32)
        scale = sb("scale", [P, BANK])
        level = sb("level", [P, BANK])
        weight = sb("weight", [P, BANK])
        wt_hi = sb("wt_hi", [P, BANK], F32R)
        wt_lo = sb("wt_lo", [P, BANK], F32R)

        qk_loaded = [sem(f"qk_loaded{i}") for i in range(2)]
        v_loaded = [sem(f"v_loaded{i}") for i in range(2)]
        score_done = sem("score_done")
        clip_done = sem("clip_done")
        low_done = sem("low_done")
        rowmax_done = sem("rowmax_done")
        negmax_done = sem("negmax_done")
        exp_done = sem("exp_done")
        turned = sem("turned")
        act_copied = sem("act_copied")
        dve_copied = sem("dve_copied")
        pv_done = sem("pv_done")
        partial_done = sem("partial_done")
        inv_done = sem("inv_done")
        fold_done = sem("fold_done")
        norm_done = sem("norm_done")
        o_stored = sem("o_stored")
        begun = sem("begun")
        passed = sem("passed")
        code_loaded = sem("code_loaded")
        restored = sem("restored")
        wt_stored = sem("wt_stored")
        block = ctx.enter_context(nc.Block())

        def copy_turned(eng, copy, act, copied, base, slot, c):
            t = slot % QT
            unit = slot // QT
            need(eng, pv_done, 2 * HALVES * base + unit - 1)
            for g in range(GROUPS):
                if on_act(t, g) == act:
                    eng.wait_ge(turned, GROUPS * c + g + 1)
                    copy(probT[unit % 2][:, 4 * g:4 * g + 4, P * t:P * (t + 1)],
                         ps[:, 4 + g % 2, :].rearrange("p (i q) -> p i q", q=P)).then_inc(copied, 1)

        @block.gpsimd
        def _(pool):
            def restore(n, q_ap, s_ap, hi_ap, lo_ap):
                pool.dma_start(code[:, :], q_ap).then_inc(code_loaded, 16)
                pool.dma_start(scale[:, :], s_ap.partition_broadcast(P)).then_inc(code_loaded, 16)
                wait_alone(pool, code_loaded, 32 * n + 32, passed)
                pool.tensor_scalar(level[:, :], code[:, :], 1.0, -ZERO_POINT, ALU.mult, ALU.add).then_inc(restored, 1)
                wait_alone(pool, restored, 4 * n + 1, passed)
                pool.tensor_tensor(weight[:, :], level[:, :], scale[:, :], ALU.mult).then_inc(restored, 1)
                wait_alone(pool, restored, 4 * n + 2, passed)
                pool.tensor_copy(wt_hi[:, :], weight[:, :]).then_inc(restored, 1)
                wait_alone(pool, restored, 4 * n + 3, passed)
                pool.tensor_tensor(wt_lo[:, :], weight[:, :], wt_hi[:, :].bitcast(F32), ALU.subtract) \
                    .then_inc(restored, 1)
                wait_alone(pool, restored, 4 * n + 4, passed)
                pool.dma_start(hi_ap, wt_hi[:, :].bitcast(F32)).then_inc(wt_stored, 16)
                pool.dma_start(lo_ap, wt_lo[:, :].bitcast(F32)).then_inc(wt_stored, 16)
                wait_alone(pool, wt_stored, 32 * n + 32, passed)

            pool.memset(weight[:, :], 0.0).then_inc(begun, 1)
            K1, N1 = w1_q.shape[0] // P, w1_q.shape[1] // BANK
            with pool.Fori(0, K1) as kt:
                for n in range(N1):
                    cols = slice(BANK * n, BANK * (n + 1))
                    r = bass.ds(P * kt, P)
                    restore(N1 * kt + n, w1_q[r, cols], w1_s[bass.ds(kt, 1), cols].rearrange("a n -> (a n)"),
                            w1_d[0][r, cols], w1_d[1][r, cols])
            with pool.Fori(0, w2_q.shape[0] // P) as kt:
                r = bass.ds(P * kt, P)
                restore(K1 * N1 + kt, w2_q[r, :], w2_s[bass.ds(kt, 1), :].rearrange("a n -> (a n)"),
                        w2_d[0][r, :], w2_d[1][r, :])

        @block.sync
        def _(sp):
            def step(base, slot):
                if (n := at(base, slot, 1, 2, N_HEADS)) is not None:
                    par = (slot - 1) % 2
                    need(sp, pv_done, 2 * (n - 1))
                    sp.dma_start(v_head[par][:, :, :].rearrange("p t d -> p (t d)"),
                                 v_d[bass.ds(n, 1)].rearrange("h p n -> (h p) n")).then_inc(v_loaded[par], 16)
                if (n := at(base, slot, 0, 2, N_HEADS)) is not None:
                    need(sp, score_done, 2 * PER_HEAD * (n - 1))
                    r = bass.ds(D * n, D)
                    for g in range(4):
                        sp.dma_start(k_stack[slot][D * g:D * (g + 1), :].bitcast(F32), kT_d[g % 2][r, :]) \
                            .then_inc(qk_loaded[slot], 16)
                        sp.dma_start(q_stack[slot][D * g:D * (g + 1), :].bitcast(F32), qT_d[g // 2][r, :]) \
                            .then_inc(qk_loaded[slot], 16)

            run_steps(sp, step, N_HEADS, 2, first=2, tail=1)

        @block.tensor
        def _(pe):
            def scores(base, slot, s, half):
                par = slot // PER_HEAD
                rows = slice(P * (slot % PER_HEAD), P * (slot % PER_HEAD + 1))
                need(pe, clip_done, 2 * (s - 1) + half + 1)
                for n in (2 * half, 2 * half + 1):
                    mm = pe.matmul(ps[:, n, :], q_stack[par][:, rows], k_stack[par][:, BANK * n:BANK * (n + 1)],
                                   start=True, stop=True)
                mm.then_inc(score_done, 1)

            def turn(base, slot, g):
                pg, pslot = (g - 2, slot) if g >= 2 else (g + 2, slot - 1)
                act = on_act(pslot % 2, pg)
                need(pe, act_copied if act else dve_copied, copies(act, base, pslot, pg))
                for i in range(4):
                    kv = 4 * g + i
                    mm = pe.transpose(ps[:, 4 + g % 2, P * i:P * (i + 1)], prob[slot % 4][:, P * kv:P * (kv + 1)],
                                      A["ident"][:, :])
                mm.then_inc(turned, 1)

            def step(base, slot):
                s = at(base, slot, SCORE, UNROLL, STEPS)
                c = at(base, slot, TURN, UNROLL, STEPS)
                if s is not None:
                    if slot % PER_HEAD == 0:
                        pe.wait_ge(qk_loaded[slot // PER_HEAD], 128 * base + 128)
                    scores(base, slot, s, 0)
                if c is not None:
                    pe.wait_ge(exp_done, c + 1)
                    turn(base, slot - TURN, 0)
                    turn(base, slot - TURN, 1)
                if s is not None:
                    scores(base, slot, s, 1)
                if c is not None:
                    turn(base, slot - TURN, 2)
                    turn(base, slot - TURN, 3)
                if (c := at(base, slot, PV, UNROLL, STEPS)) is not None:
                    lane = slot - PV
                    unit, quarter = lane // QT, lane % QT
                    par = unit // HALVES % 2
                    if quarter == 0:
                        pe.wait_ge(act_copied, copies(True, base, lane + QT - 1, GROUPS - 1))
                        pe.wait_ge(dve_copied, copies(False, base, lane + QT - 1, GROUPS - 1))
                        pe.wait_ge(v_loaded[par], 16 * (base + unit // (2 * HALVES)) + 16)
                        need(pe, partial_done, 2 * HALVES * base + unit)
                    for g in range(4):
                        kv = 4 * quarter + g
                        mm = pe.matmul(ps[D * g:D * (g + 1), 6, :], v_head[par][:, kv, :],
                                       probT[unit % 2][:, kv, :], start=(quarter == 0), stop=(quarter == QT - 1))
                    if quarter == QT - 1:
                        mm.then_inc(pv_done, 1)
                if (slot - FOLD) % QT == 0 and at(base, slot, FOLD, UNROLL, STEPS) is not None:
                    unit = 2 * HALVES * base + (slot - FOLD) // QT
                    pe.wait_ge(partial_done, unit + 1)
                    need(pe, norm_done, unit)
                    for t in range(QT):
                        mm = pe.matmul(ps[:, 7, D * t:D * (t + 1)], partial[:, P * t:P * (t + 1)], A["fold"][:, :],
                                       start=True, stop=True)
                    mm.then_inc(fold_done, 1)

            run_steps(pe, step, STEPS, UNROLL, first=1, tail=NORM)

        @block.scalar
        def _(act):
            def step(base, slot):
                if (c := at(base, slot, TURN, UNROLL, STEPS)) is not None:
                    copy_turned(act, act.copy, True, act_copied, base, slot - TURN, c)
                if (s := at(base, slot, SCORE, UNROLL, STEPS)) is not None:
                    act.wait_ge(negmax_done, s + 1)
                    need(act, turned, GROUPS * (s - 3))
                    act.activation(prob[slot % 4][:, :], score[slot % 2][:, :], ACT.Exp,
                                   bias=neg_max[:, slot % 4:slot % 4 + 1], scale=1.0,
                                   accum_out=row_sum[:, slot:slot + 1]).then_inc(exp_done, 1)
                if slot == NORM - 3 and (isinstance(base, int) is False or base > 0):
                    act.wait_ge(norm_done, 2 * HALVES * base)
                    act.dma_start(o_d[bass.ds(base - 1, 1)].rearrange("a p n -> (a p) n"),
                                  o_pair[:, :, :].rearrange("p t n -> p (t n)")).then_inc(o_stored, 16)

            run_steps(act, step, STEPS, UNROLL, first=1, tail=NORM)
            act.wait_ge(o_stored, 16 * (STEPS // UNROLL))

        def softmax_steps(dve, clipping):
            def clip(slot, s, half):
                dve.wait_ge(score_done, 2 * s + half + 1)
                need(dve, exp_done, s - 1)
                need(dve, negmax_done, s - 1)
                dst = score[slot % 2][:, 2 * BANK * half:2 * BANK * (half + 1)]
                src = ps[:, 2 * half:2 * half + 2, :].rearrange("p b n -> p (b n)")
                high = A["clip_high"][:, 0:1] if clipping else CLAMP
                dve.tensor_scalar(dst, src, high, None, ALU.min, ALU.max,
                                  accum_out=half_max[:, slot % 2, half:half + 1]).then_inc(clip_done, 1)

            def step(base, slot):
                s = at(base, slot, SCORE, UNROLL, STEPS)
                if s is not None:
                    clip(slot, s, 0)
                if (slot - PART) % QT == 0 and at(base, slot, PART, UNROLL, STEPS) is not None:
                    lane = (slot - PART) // QT
                    unit = 2 * HALVES * base + lane
                    dve.wait_ge(pv_done, unit + 1)
                    need(dve, fold_done, unit)
                    dve.tensor_copy(partial[:, :], ps[:, 6, :]).then_inc(partial_done, 1)
                    dve.wait_ge(exp_done, QT * unit + QT)
                    need(dve, norm_done, unit - 1)
                    first = (QT * lane) % UNROLL
                    dve.reciprocal(inv_sum[:, lane % 2, :], row_sum[:, first:first + QT]).then_inc(inv_done, 1)
                if s is not None:
                    clip(slot, s, 1)
                    dve.wait_ge(clip_done, 2 * s + 2)
                    pair = half_max[:, slot % 2, :]
                    if not clipping:
                        dve.tensor_scalar(neg_max[:, slot % 4:slot % 4 + 1], pair[:, 0:1], pair[:, 1:2], -1.0,
                                          ALU.max, ALU.mult).then_inc(negmax_done, 1)
                    else:
                        dve.tensor_scalar(score[slot % 2][:, :], score[slot % 2][:, :], A["clip_low"][:, 0:1], None,
                                          ALU.max).then_inc(low_done, 1)
                        dve.tensor_scalar(row_max[:, slot % 2:slot % 2 + 1], pair[:, 0:1], pair[:, 1:2], None,
                                          ALU.max).then_inc(rowmax_done, 1)
                        dve.wait_ge(rowmax_done, s + 1)
                        dve.wait_ge(low_done, s + 1)
                        dve.tensor_scalar(neg_max[:, slot % 4:slot % 4 + 1], row_max[:, slot % 2:slot % 2 + 1],
                                          A["clip_low"][:, 0:1], -1.0, ALU.max, ALU.mult).then_inc(negmax_done, 1)
                if (c := at(base, slot, TURN, UNROLL, STEPS)) is not None:
                    copy_turned(dve, dve.tensor_copy, False, dve_copied, base, slot - TURN, c)
                if (slot - NORM) % QT == 0 and at(base, slot, NORM, UNROLL, STEPS) is not None:
                    lane = (slot - NORM) // QT
                    unit = 2 * HALVES * base + lane
                    dve.wait_ge(fold_done, unit + 1)
                    dve.wait_ge(inv_done, unit + 1)
                    at_head, half = lane // HALVES % 2, lane % HALVES
                    if lane % (2 * HALVES) == 0:
                        need(dve, o_stored, 16 * (base + lane // (2 * HALVES)))
                    dve.tensor_tensor(o_pair[:, QT * half:QT * (half + 1), D * at_head:D * (at_head + 1)],
                                      ps[:, 7, 0:QT * D].rearrange("p (t d) -> p t d", d=D),
                                      inv_sum[:, lane % 2, :].unsqueeze(2).to_broadcast([P, QT, D]),
                                      ALU.mult).then_inc(norm_done, 1)

            run_steps(dve, step, STEPS, UNROLL, first=1, tail=NORM)

        @block.vector
        def _(dve):
            clipping = dve.value_load(A["clip_path"][0:1, 0:1], min_val=0, max_val=1)
            with dve.If(clipping > 0):
                softmax_steps(dve, True)
            with dve.Else():
                softmax_steps(dve, False)


def project_out(k, A, x, o_d, wo, bo, g_attn, g_ffn, x1_d, w1_d, w2_d, w1, w2):
    nc, ps = k.nc, k.ps
    B, SQ, C = x.shape
    KT, TT = C // P, BANK // P
    CH = B * SQ // BANK
    x_rows = x.rearrange("b (t p) c -> (b t) p c", p=P)
    PAIRS = HEADS // 2
    o_rows = o_d.rearrange("(b j) p (t n) -> b j p t n", j=PAIRS, n=2 * D)

    with ExitStack() as ctx:
        sb = lambda name, shape, dt=F32: k.sb(ctx, "po_" + name, shape, dt)
        sem = lambda name: k.sem(ctx, "po_" + name)
        w_hi = sb("w_hi", [P, KT, C], F32R)
        w_lo = sb("w_lo", [P, KT, C], F32R)
        gates = sb("gates", [P, 2])
        tanhs = sb("tanhs", [P, 2])
        bias = sb("bias", [P, C])
        o_in = sb("o_in", [P, TT, C])
        x_in = [sb(f"x_in{i}", [P, TT, C]) for i in range(2)]
        oT_hi = [sb(f"oT_hi{i}", [P, KT, BANK], F32R) for i in range(2)]
        oT_lo = [sb(f"oT_lo{i}", [P, KT, BANK], F32R) for i in range(2)]
        eps = sb("eps", [P, 1])
        stats = sb("stats", [P, TT, 6])
        meanvar = sb("meanvar", [P, TT, 2])
        mv_all = sb("mv_all", [P, CH * TT, 2])
        small = sb("small", [P, 6, CH * TT])

        w_in = sem("w_in")
        big_in = sem("big_in")
        tanh_done = sem("tanh_done")
        setup = sem("setup")
        passed = sem("passed")
        o_loaded = sem("o_loaded")
        x_loaded = [sem(f"x_loaded{i}") for i in range(2)]
        o_turned = sem("o_turned")
        ohi_done = sem("ohi_done")
        olo_done = sem("olo_done")
        out_done = sem("out_done")
        biased = sem("biased")
        x1_done = sem("x1_done")
        stat_done = sem("stat_done")
        mv_done = sem("mv_done")
        kept = sem("kept")
        x1_stored = [sem(f"x1_stored{i}") for i in range(2)]
        end = sem("end")
        root = sem("root")
        block = ctx.enter_context(nc.Block())
        w_stage = x_in[1]

        @block.gpsimd
        def _(pool):
            def step(base, slot):
                if (s := at(base, slot, 0, 2, CH)) is not None:
                    pool.wait_ge(x_loaded[slot], 16 * base + 16 + (16 if slot else 0))
                    pool.tensor_tensor(x_in[slot][:, :, :], x_in[slot][:, :, :],
                                       bias[:, :].unsqueeze(1).to_broadcast([P, TT, C]), ALU.add).then_inc(biased, 1)

            pool.wait_ge(setup, 3)
            for part in range(2):
                pool.dma_start(w1[part][:, :, :].bitcast(F32), w1_d[part].rearrange("(k p) n -> p k n", p=P)) \
                    .then_inc(big_in, 16)
            for part in range(2):
                pool.dma_start(w2[part][:, :, :].bitcast(F32), w2_d[part].rearrange("(k p) n -> p k n", p=P)) \
                    .then_inc(big_in, 16)
            run_steps(pool, step, CH, 2, first=1)
            pool.wait_ge(big_in, 64)

        @block.sync
        def _(sp):
            def step(base, slot):
                if (s := at(base, slot, 0, 2, CH)) is not None:
                    need(sp, o_turned, KT * s)
                    for j in range(PAIRS):
                        sp.dma_start(o_in[:, :, 2 * D * j:2 * D * (j + 1)], o_rows[bass.ds(base, 1), j, :, TT * slot:TT * (slot + 1), :]
                                     .rearrange("a p t n -> (a p) t n")).then_inc(o_loaded, 16)
                    if slot == 1:
                        need(sp, setup, 3)
                    need(sp, x1_stored[slot], 16 * base)
                    need(sp, stat_done, TT * (s - 1))
                    sp.dma_start(x_in[slot][:, :, :], x_rows[bass.ds(TT * s, TT)].rearrange("t p c -> p t c")) \
                        .then_inc(x_loaded[slot], 16)
                if (c := at(base, slot, 1, 2, CH)) is not None:
                    par = (slot - 1) % 2
                    sp.wait_ge(x1_done, TT * c + TT)
                    sp.dma_start(x1_d[bass.ds(TT * c, TT)].rearrange("t p c -> p t c"), x_in[par][:, :, :]) \
                        .then_inc(x1_stored[par], 16)

            sp.dma_start(w_stage[:, :, :], wo.rearrange("(k p) n -> p k n", p=P)).then_inc(x_loaded[1], 16)
            sp.dma_start(gates[:, 0:1], g_attn.partition_broadcast(P)).then_inc(w_in, 16)
            sp.dma_start(gates[:, 1:2], g_ffn.partition_broadcast(P)).then_inc(w_in, 16)
            sp.dma_start(bias[:, :], bo.partition_broadcast(P)).then_inc(w_in, 16)
            run_steps(sp, step, CH, 2, first=1, tail=1)
            for i in range(2):
                sp.wait_ge(x1_stored[i], 16 * (CH // 2))

        @block.tensor
        def _(pe):
            def step(base, slot):
                if (s := at(base, slot, 0, 2, CH)) is not None:
                    pe.wait_ge(o_loaded, 16 * PAIRS * (s + 1))
                    for kt in range(KT):
                        need(pe, olo_done, KT * (s - 1) + kt + 1)
                        for t in range(TT):
                            mm = pe.transpose(ps[:, kt, P * t:P * (t + 1)], o_in[:, t, P * kt:P * (kt + 1)],
                                              A["ident"][:, :])
                        mm.then_inc(o_turned, 1)
                if (c := at(base, slot, 1, 2, CH)) is not None:
                    par = (slot - 1) % 2
                    pe.wait_ge(ohi_done, KT * c + KT)
                    pe.wait_ge(olo_done, KT * c + KT)
                    for t in range(TT):
                        need(pe, x1_done, TT * (c - 1) + t + 1)
                        parts = [(a, b, kt) for kt in range(KT)
                                 for a, b in ((oT_hi, w_hi), (oT_hi, w_lo), (oT_lo, w_hi))]
                        for n, (a, b, kt) in enumerate(parts):
                            mm = pe.matmul(ps[:, 4 + t, :], a[par][:, kt, P * t:P * (t + 1)], b[:, kt, :],
                                           start=(n == 0), stop=(n == len(parts) - 1))
                        mm.then_inc(out_done, 1)

            pe.wait_ge(setup, 2)
            run_steps(pe, step, CH, 2, first=2, tail=1)

        @block.scalar
        def _(act):
            def step(base, slot):
                if (s := at(base, slot, 0, 2, CH)) is not None:
                    need(act, out_done, TT * (s - 1))
                    for kt in range(KT):
                        act.wait_ge(o_turned, KT * s + kt + 1)
                        act.activation(oT_hi[slot][:, kt, :], ps[:, kt, :], ACT.Identity).then_inc(ohi_done, 1)

            act.wait_ge(w_in, 48)
            act.activation(tanhs[:, :], gates[:, :], ACT.Tanh).then_inc(tanh_done, 1)
            run_steps(act, step, CH, 2, first=2)
            act.wait_ge(end, 2)
            act.activation(small[:, 1, :], small[:, 0, :], ACT.Sqrt, bias=eps[:, 0:1]).then_inc(root, 1)
            act.wait_ge(end, 5)
            act.activation(A["root2"][:, :], small[:, 4, :], ACT.Sqrt, bias=eps[:, 0:1]).then_inc(root, 1)

        @block.vector
        def _(dve):
            def step(base, slot):
                if (s := at(base, slot, 0, 2, CH)) is not None:
                    need(dve, out_done, TT * (s - 1))
                    for kt in range(KT):
                        dve.wait_ge(ohi_done, KT * s + kt + 1)
                        dve.tensor_tensor(oT_lo[slot][:, kt, :], ps[:, kt, :], oT_hi[slot][:, kt, :].bitcast(F32),
                                          ALU.subtract).then_inc(olo_done, 1)
                if (c := at(base, slot, 1, 2, CH)) is not None:
                    par = (slot - 1) % 2
                    dve.wait_ge(biased, c + 1)
                    for t in range(TT):
                        dve.wait_ge(out_done, TT * c + t + 1)
                        dve.scalar_tensor_tensor(x_in[par][:, t, :], ps[:, 4 + t, :], tanhs[:, 0:1],
                                                 x_in[par][:, t, :], ALU.mult, ALU.add).then_inc(x1_done, 1)
                    need(dve, mv_done, TT * c)
                    for t in range(TT):
                        dve.wait_ge(x1_done, TT * c + t + 1)
                        dve.bn_stats(stats[:, t, :], x_in[par][:, t, :]).then_inc(stat_done, 1)
                    need(dve, kept, c)
                    for t in range(TT):
                        wait_alone(dve, stat_done, TT * c + t + 1, passed)
                        dve.bn_aggr(meanvar[:, t, :], stats[:, t, :]).then_inc(mv_done, 1)
                    dve.wait_ge(mv_done, TT * c + TT)
                    dve.tensor_copy(mv_all[:, bass.ds(TT * c, TT), :], meanvar[:, :, :]).then_inc(kept, 1)

            dve.wait_ge(x_loaded[1], 16)
            dve.tensor_copy(w_hi[:, :, :], w_stage[:, :, :]).then_inc(setup, 1)
            dve.wait_ge(setup, 1)
            dve.tensor_tensor(w_lo[:, :, :], w_stage[:, :, :], w_hi[:, :, :].bitcast(F32), ALU.subtract) \
                .then_inc(setup, 1)
            dve.wait_ge(tanh_done, 1)
            dve.wait_ge(w_in, 48)
            dve.tensor_scalar(bias[:, :], bias[:, :], tanhs[:, 0:1], None, ALU.mult).then_inc(setup, 1)
            run_steps(dve, step, CH, 2, first=2, tail=1)
            dve.memset(eps[:, :], EPS).then_inc(end, 1)
            dve.wait_ge(kept, CH)
            dve.tensor_copy(small[:, 0, :], mv_all[:, :, 1]).then_inc(end, 1)
            dve.tensor_copy(A["mean1"][:, :], mv_all[:, :, 0]).then_inc(end, 1)
            dve.wait_ge(root, 1)
            dve.reciprocal(small[:, 2, :], small[:, 1, :]).then_inc(end, 1)
            dve.wait_ge(end, 4)
            dve.tensor_tensor(small[:, 3, :], small[:, 0, :], small[:, 2, :], ALU.mult).then_inc(root, 1)
            dve.wait_ge(root, 2)
            dve.tensor_tensor(small[:, 4, :], small[:, 3, :], small[:, 2, :], ALU.mult).then_inc(end, 1)
            dve.wait_ge(root, 3)
            dve.reciprocal(small[:, 5, :], A["root2"][:, :]).then_inc(end, 1)
            dve.wait_ge(end, 6)
            dve.tensor_tensor(A["norm12"][:, :], small[:, 2, :], small[:, 5, :], ALU.mult).then_inc(end, 1)
            dve.tensor_scalar(A["keep2"][:, :], A["root2"][:, :], tanhs[:, 1:2], None, ALU.mult).then_inc(end, 1)
            dve.tensor_scalar(A["half_gate"][:, :], tanhs[:, 1:2], 0.5, None, ALU.mult).then_inc(end, 1)


def feed_forward(k, A, x1_d, w1, w2, gamma, beta, b1, b2, out):
    nc, ps = k.nc, k.ps
    R, _, C = x1_d.shape
    KT, TT = C // P, BANK // P
    F = w1[0].shape[2]
    FT = F // P
    CH = R // TT
    UNROLL = 2 * FT
    STEPS = CH * FT
    LAG = 2
    out_rows = out.rearrange("b (t p) c -> (b t) p c", p=P)

    with ExitStack() as ctx:
        sb = lambda name, shape, dt=F32: k.sb(ctx, "ff_" + name, shape, dt)
        sem = lambda name: k.sem(ctx, "ff_" + name)
        gam = sb("gam", [P, KT])
        bet = sb("bet", [P, KT])
        b1_t = sb("b1_t", [P, FT])
        b2_raw = sb("b2_raw", [P, C])
        b2_half = sb("b2_half", [P, C])
        x_in = [sb(f"x_in{i}", [P, TT, C]) for i in range(2)]
        coef = sb("coef", [P, 3, TT])
        normed = sb("normed", [P, TT, C])
        h = sb("h", [P, KT, BANK])
        h_hi = sb("h_hi", [P, KT, BANK], F32R)
        h_lo = sb("h_lo", [P, KT, BANK], F32R)
        y = [sb(f"y{i}", [P, BANK]) for i in range(2)]
        y_hi = [sb(f"y_hi{i}", [P, BANK], F32R) for i in range(2)]
        y_lo = [sb(f"y_lo{i}", [P, BANK], F32R) for i in range(2)]

        c_in = sem("c_in")
        setup = sem("setup")
        passed = sem("passed")
        x_loaded = [sem(f"x_loaded{i}") for i in range(2)]
        coef_done = sem("coef_done")
        normed_done = sem("normed_done")
        kept_done = sem("kept_done")
        base_done = sem("base_done")
        h_turned = sem("h_turned")
        h_done = sem("h_done")
        hhi_done = sem("hhi_done")
        hlo_done = sem("hlo_done")
        first_done = sem("first_done")
        y_done = sem("y_done")
        yhi_done = sem("yhi_done")
        ylo_done = sem("ylo_done")
        second_done = sem("second_done")
        out_done = sem("out_done")
        out_stored = [sem(f"out_stored{i}") for i in range(2)]
        block = ctx.enter_context(nc.Block())

        def next_chunk(base, slot, ahead=0):
            c = 2 * base + (slot + ahead) // FT + (0 if ahead else 1)
            return None if isinstance(c, int) and c >= CH else c

        @block.sync
        def _(sp):
            def step(base, slot):
                c = 2 * base + slot
                sp.wait_ge(out_done, TT * c + TT)
                sp.dma_start(out_rows[bass.ds(TT * c, TT)].rearrange("t p c -> p t c"), x_in[slot][:, :, :]) \
                    .then_inc(out_stored[slot], 16)
                if not isinstance(c, int) or c + 2 < CH:
                    sp.wait_ge(out_stored[slot], 16 * base + 16)
                    load(slot, c + 2)

            def load(par, c):
                sp.dma_start(x_in[par][:, :, :], x1_d[bass.ds(TT * c, TT)].rearrange("t p c -> p t c")) \
                    .then_inc(x_loaded[par], 16)

            load(0, 0)
            for dst, src in ((gam, gamma), (bet, beta), (b1_t, b1)):
                sp.dma_start(dst[:, :], src.rearrange("(m p) -> p m", p=P),
                             allow_slow_non_contiguous=True).then_inc(c_in, 16)
            sp.dma_start(b2_raw[:, :], b2.partition_broadcast(P)).then_inc(c_in, 16)
            load(1, 1)
            run_steps(sp, step, CH, 2, first=1, last=1)
            for i in range(2):
                sp.wait_ge(out_stored[i], 16 * (CH // 2))

        def turn(pe, c):
            pe.wait_ge(normed_done, TT * c + TT)
            for kt in range(KT):
                need(pe, h_done, KT * c + kt - 1)
                for t in range(TT):
                    mm = pe.transpose(ps[:, 6 + kt % 2, P * t:P * (t + 1)], normed[:, t, P * kt:P * (kt + 1)],
                                      A["ident"][:, :])
                mm.then_inc(h_turned, 1)

        @block.tensor
        def _(pe):
            def step(base, slot):
                if (s := at(base, slot, 0, UNROLL, STEPS)) is not None:
                    f = slot % FT
                    if f == 0:
                        c = 2 * base + slot // FT
                        pe.wait_ge(hhi_done, KT * c + KT)
                        pe.wait_ge(hlo_done, KT * c + KT)
                    need(pe, y_done, s - 1)
                    parts = [(a, b, kt) for kt in range(KT) for a, b in ((0, h_hi), (1, h_hi), (0, h_lo))]
                    for n, (a, b, kt) in enumerate(parts):
                        mm = pe.matmul(ps[:, 4 + f % 2, :], w1[a][:, kt, P * f:P * (f + 1)], b[:, kt, :],
                                       start=(n == 0), stop=(n == len(parts) - 1))
                    mm.then_inc(first_done, 1)
                    if f == FT - 1 and (c := next_chunk(base, slot)) is not None:
                        turn(pe, c)
                if (e := at(base, slot, LAG, UNROLL, STEPS)) is not None:
                    f = (slot - LAG) % FT
                    chunk = 2 * base + (slot - LAG) // FT
                    pe.wait_ge(ylo_done, e + 1)
                    for t in range(TT):
                        if f == 0:
                            need(pe, out_done, TT * (chunk - 1) + t + 1)
                        cols = slice(P * t, P * (t + 1))
                        parts = ((y_hi, 0), (y_hi, 1), (y_lo, 0))
                        for n, (a, b) in enumerate(parts):
                            mm = pe.matmul(ps[:, t, :], a[f % 2][:, cols], w2[b][:, f, :],
                                           start=(f == 0 and n == 0), stop=(f == FT - 1 and n == 2))
                    mm.then_inc(second_done, 1)

            turn(pe, 0)
            run_steps(pe, step, STEPS, UNROLL, first=1, last=1, tail=LAG)

        def shape_h(act, c):
            for kt in range(KT):
                act.wait_ge(h_turned, KT * c + kt + 1)
                need(act, hlo_done, KT * (c - 1) + kt + 1)
                act.activation(h[:, kt, :], ps[:, 6 + kt % 2, :], ACT.Identity, bias=bet[:, kt:kt + 1],
                               scale=gam[:, kt:kt + 1]).then_inc(h_done, 1)

        @block.scalar
        def _(act):
            def step(base, slot):
                if (s := at(base, slot, 0, UNROLL, STEPS)) is not None:
                    f = slot % FT
                    act.wait_ge(first_done, s + 1)
                    need(act, ylo_done, s - 1)
                    act.activation(y[f % 2][:, :], ps[:, 4 + f % 2, :], ACT.Silu, bias=b1_t[:, f:f + 1]) \
                        .then_inc(y_done, 1)
                    if f == FT - 1 and (c := next_chunk(base, slot)) is not None:
                        shape_h(act, c)

            act.wait_ge(c_in, 64)
            shape_h(act, 0)
            run_steps(act, step, STEPS, UNROLL, first=1, last=1)

        @block.gpsimd
        def _(pool):
            def step(base, slot):
                c = 2 * base + slot
                pool.wait_ge(kept_done, TT * c + TT)
                pool.tensor_tensor(x_in[slot][:, :, :], x_in[slot][:, :, :],
                                   b2_half[:, :].unsqueeze(1).to_broadcast([P, TT, C]), ALU.add).then_inc(base_done, 1)

            pool.wait_ge(setup, 1)
            run_steps(pool, step, CH, 2, first=1)

        @block.vector
        def _(dve):
            def coefs(par, loads, c):
                dve.wait_ge(x_loaded[par], 16 * loads)
                need(dve, normed_done, TT * c)
                need(dve, kept_done, TT * c)
                for i, src in enumerate(("mean1", "norm12", "keep2")):
                    dve.tensor_copy(coef[:, i, :], A[src][:, bass.ds(TT * c, TT)]).then_inc(coef_done, 1)

            def norm(par, c, t):
                dve.wait_ge(coef_done, 3 * c + 3)
                if t == 0:
                    need(dve, h_turned, KT * c)
                dve.tensor_scalar(normed[:, t, :], x_in[par][:, t, :], coef[:, 0, t:t + 1], coef[:, 1, t:t + 1],
                                  ALU.subtract, ALU.mult).then_inc(normed_done, 1)
                dve.wait_ge(normed_done, TT * c + t + 1)
                dve.scalar_tensor_tensor(x_in[par][:, t, :], normed[:, t, :], coef[:, 2, t:t + 1],
                                         x_in[par][:, t, :], ALU.mult, ALU.add).then_inc(kept_done, 1)

            def split_h(c):
                need(dve, first_done, FT * c)
                for kt in range(KT):
                    dve.wait_ge(h_done, KT * c + kt + 1)
                    dve.tensor_copy(h_hi[:, kt, :], h[:, kt, :]).then_inc(hhi_done, 1)
                    dve.wait_ge(hhi_done, KT * c + kt + 1)
                    dve.tensor_tensor(h_lo[:, kt, :], h[:, kt, :], h_hi[:, kt, :].bitcast(F32),
                                      ALU.subtract).then_inc(hlo_done, 1)

            def step(base, slot):
                if (s := at(base, slot, 0, UNROLL, STEPS)) is not None:
                    f = slot % FT
                    dve.wait_ge(y_done, s + 1)
                    need(dve, second_done, s - 1)
                    dve.tensor_copy(y_hi[f % 2][:, :], y[f % 2][:, :]).then_inc(yhi_done, 1)
                    dve.wait_ge(yhi_done, s + 1)
                    dve.tensor_tensor(y_lo[f % 2][:, :], y[f % 2][:, :], y_hi[f % 2][:, :].bitcast(F32),
                                      ALU.subtract).then_inc(ylo_done, 1)
                    c = next_chunk(base, slot)
                    if c is not None:
                        par, loads = (slot // FT + 1) % 2, base + 1 + (slot // FT)
                        if f == 7:
                            coefs(par, loads, c)
                        if 8 <= f < 8 + TT:
                            norm(par, c, f - 8)
                        if f == FT - 1:
                            split_h(c)
                if (slot - LAG) % FT == FT - 1 and at(base, slot, LAG, UNROLL, STEPS) is not None:
                    chunk = 2 * base + (slot - LAG) // FT
                    par = (slot - LAG) // FT % 2
                    dve.wait_ge(second_done, FT * chunk + FT)
                    dve.wait_ge(base_done, chunk + 1)
                    for t in range(TT):
                        dve.scalar_tensor_tensor(x_in[par][:, t, :], ps[:, t, :], A["half_gate"][:, 0:1],
                                                 x_in[par][:, t, :], ALU.mult, ALU.add).then_inc(out_done, 1)

            dve.wait_ge(c_in, 64)
            dve.tensor_scalar(b2_half[:, :], b2_raw[:, :], A["half_gate"][:, 0:1], None, ALU.mult).then_inc(setup, 1)
            coefs(0, 1, 0)
            for t in range(TT):
                norm(0, 0, t)
            split_h(0)
            run_steps(dve, step, STEPS, UNROLL, first=1, last=1, tail=LAG)


def gated_cross_attention_block(nc, x, ctx_768, g_xattn, g_ffn, wq, bq, wk, bk, wv, bv, wo, bo,
                                ln_gamma, ln_beta, fc1_q, fc1_scales, fc1_bias, fc2_q, fc2_scales, fc2_bias, out):
    B, SQ, C = x.shape
    SK = ctx_768.shape[1]
    F = fc1_q.shape[1]
    ROWS = B * SQ // P

    def dram(name, shape):
        return nc.dram_tensor(name, shape, F32, kind="Internal").ap()

    qT_d = [dram(f"qT_{part}", (B * C, SQ)) for part in ("hi", "lo")]
    kT_d = [dram(f"kT_{part}", (B * C, SK)) for part in ("hi", "lo")]
    v_d = dram("v_heads", (B * HEADS, P, SK // P * D))
    o_d = dram("o_pairs", (B * HEADS // 2, P, SQ // P * 2 * D))
    w1_d = [dram(f"w1_{part}", (C, F)) for part in ("hi", "lo")]
    w2_d = [dram(f"w2_{part}", (F, C)) for part in ("hi", "lo")]
    x1_d = dram("x1", (ROWS, P, C))

    with ExitStack() as ctx:
        k = Core(nc, ctx)
        A = {name: k.sb(ctx, name, shape, dt) for name, shape, dt in (
            ("ident", [P, P], F32), ("fold", [P, D], F32), ("clip_path", [1, 1], I32), ("clip_high", [P, 1], F32),
            ("clip_low", [P, 1], F32), ("mean1", [P, ROWS], F32), ("root2", [P, ROWS], F32),
            ("norm12", [P, ROWS], F32), ("keep2", [P, ROWS], F32), ("half_gate", [P, 1], F32))}
        with ExitStack() as bounds:
            A |= {name: k.sb(bounds, name, [P, BANK]) for name in ("q_sq_sum", "k_sq_sum", "not_finite")}
            project_queries(k, A, x, wq, bq, qT_d)
            project_keys_values(k, A, ctx_768, wk, bk, wv, bv, kT_d, v_d)
        attend(k, A, (B, SQ, SK), qT_d, kT_d, v_d, o_d, fc1_q, fc1_scales, fc2_q, fc2_scales, w1_d, w2_d)
        w1 = [k.sb(ctx, f"w1_sb{i}", [P, C // P, F], F32R) for i in range(2)]
        w2 = [k.sb(ctx, f"w2_sb{i}", [P, F // P, C], F32R) for i in range(2)]
        project_out(k, A, x, o_d, wo, bo, g_xattn, g_ffn, x1_d, w1_d, w2_d, w1, w2)
        feed_forward(k, A, x1_d, w1, w2, ln_gamma, ln_beta, fc1_bias, fc2_bias, out)


_INS = ['x', 'ctx_768', 'g_xattn', 'g_ffn', 'L0_xattn_Wq', 'L0_xattn_bq', 'L0_xattn_Wk', 'L0_xattn_bk',
        'L0_xattn_Wv', 'L0_xattn_bv', 'L0_xattn_Wo', 'L0_xattn_bo', 'L0_ffn_ln_gamma', 'L0_ffn_ln_beta',
        'L0_ffn_fc1_q', 'L0_ffn_fc1_scales', 'L0_ffn_fc1_bias', 'L0_ffn_fc2_q', 'L0_ffn_fc2_scales',
        'L0_ffn_fc2_bias']
_OUTS = [((4, 1024, 512), 'float32')]


def kernel(**inputs):
    import numpy as _np
    import concourse.bacc as _bacc
    from concourse import mybir as _mybir
    from concourse.bass_utils import run_bass_kernel_spmd as _run

    nc = _bacc.Bacc("TRN2", target_bir_lowering=False, num_devices=1)
    arrays, args = {}, []
    for name in _INS:
        a = _np.ascontiguousarray(inputs[name])
        arrays[f"in_{name}_dram"] = a
        args.append(nc.dram_tensor(f"in_{name}_dram", a.shape, _mybir.dt.from_np(a.dtype), kind="ExternalInput").ap())
    for i, (shape, dtype) in enumerate(_OUTS):
        dt = _mybir.dt.from_np(_np.dtype(dtype))
        args.append(nc.dram_tensor(f"out_{i}_dram", shape, dt, kind="ExternalOutput").ap())
    gated_cross_attention_block(nc, *args)
    r = _run(nc, [arrays], core_ids=[0])
    got = tuple(r.results[0][f"out_{i}_dram"] for i in range(len(_OUTS)))
    return got[0]
```

```python
from contextlib import ExitStack

import concourse.bass as bass
from concourse import mybir

ALU = mybir.AluOpType
ACT = mybir.ActivationFunctionType
AX_X = mybir.AxisListType.X
F32 = mybir.dt.float32
F32R = mybir.dt.float32r
I32 = mybir.dt.int32

P = 128
BANK = 512
HEADS = 16
D = 32
CLAMP = 10000.0
EPS = 1e-5
ZERO_POINT = 128.0



def need(eng, sem, value):
    if isinstance(value, int) and value <= 0:
        return
    eng.wait_ge(sem, value)


def wait_alone(eng, sem, value, passed):
    eng.wait_ge(sem, value)
    eng.sem_inc(passed, 1)


def at(base, slot, lag, unroll, total):
    item = unroll * base + (slot - lag)
    if isinstance(item, int) and not 0 <= item < total:
        return None
    return item


def run_steps(eng, step, total, unroll, first=1, last=0, tail=0):
    bodies = total // unroll
    for base in range(first):
        for slot in range(unroll):
            step(base, slot)
    with eng.Fori(first, bodies - last) as base:
        for slot in range(unroll):
            step(base, slot)
    for s in range((bodies - last) * unroll, total + tail):
        step(s // unroll, s % unroll)


class Core:

    def __init__(self, nc, ctx):
        self.nc, self.ctx = nc, ctx
        self.ps = ctx.enter_context(nc.psum_tensor("ps", [P, 8, BANK], F32))

    def sb(self, ctx, name, shape, dt=F32):
        return ctx.enter_context(self.nc.sbuf_tensor(name, shape, dt))

    def sem(self, ctx, name):
        return ctx.enter_context(self.nc.semaphore(name))


def add_squares(pool, part, square, total, tiles, c, part_done, bound_done):
    for m in range(tiles):
        pool.wait_ge(part_done, tiles * c + m + 1)
        tile = part[:, m, :].bitcast(F32)
        need(pool, bound_done, 2 * (tiles * c + m))
        pool.tensor_tensor(square[:, :], tile, tile, ALU.mult).then_inc(bound_done, 1)
        pool.wait_ge(bound_done, 2 * (tiles * c + m) + 1)
        pool.tensor_tensor(total[:, :], total[:, :], square[:, :], ALU.add).then_inc(bound_done, 1)


def project_queries(k, A, x, wq, bq, qT_d):
    nc, ps = k.nc, k.ps
    B, SQ, C = x.shape
    KT = C // P
    CH = B * SQ // BANK
    PER = SQ // BANK
    TT = BANK // P
    SCALE = float(D) ** -0.5
    x_rows = x.rearrange("b (t p) c -> (b t) p c", p=P)

    with ExitStack() as ctx:
        sb = lambda name, shape, dt=F32: k.sb(ctx, "pq_" + name, shape, dt)
        sem = lambda name: k.sem(ctx, "pq_" + name)
        w = sb("w", [P, KT, C])
        w_hi = sb("w_hi", [P, KT, C], F32R)
        w_lo = sb("w_lo", [P, KT, C], F32R)
        bias_raw = sb("bias_raw", [P, KT])
        bias = sb("bias", [P, KT])
        eps = sb("eps", [P, 1])
        x_in = [sb(f"x_in{i}", [P, TT, C]) for i in range(2)]
        stats = sb("stats", [P, TT, 6])
        meanvar = sb("meanvar", [P, TT, 2])
        std = sb("std", [P, TT])
        rstd = sb("rstd", [P, TT])
        xT_hi = [sb(f"xT_hi{i}", [P, KT, BANK], F32R) for i in range(2)]
        xT_lo = [sb(f"xT_lo{i}", [P, KT, BANK], F32R) for i in range(2)]
        q_hi = [sb(f"q_hi{i}", [P, KT, BANK], F32R) for i in range(2)]
        q_lo = [sb(f"q_lo{i}", [P, KT, BANK], F32R) for i in range(2)]

        square = sb("square", [P, BANK])

        w_in = sem("w_in")
        setup = sem("setup")
        passed = sem("passed")
        const = sem("const")
        x_loaded = [sem(f"x_loaded{i}") for i in range(2)]
        stat_done = sem("stat_done")
        mv_done = sem("mv_done")
        std_done = sem("std_done")
        rstd_done = sem("rstd_done")
        norm_done = sem("norm_done")
        x_turned = sem("x_turned")
        xhi_done = sem("xhi_done")
        xlo_done = sem("xlo_done")
        q_done = sem("q_done")
        qhi_done = sem("qhi_done")
        qlo_done = sem("qlo_done")
        bound_done = sem("bound_done")
        finite_done = sem("finite_done")
        q_stored = [sem(f"q_stored{i}") for i in range(2)]
        block = ctx.enter_context(nc.Block())

        @block.gpsimd
        def _(pool):
            pool.memset(A["ident"][:, :], 0.0).then_inc(const, 1)
            pool.memset(A["fold"][:, :], 0.0).then_inc(const, 1)
            pool.memset(A["q_sq_sum"][:, :], 0.0).then_inc(const, 1)
            pool.memset(A["k_sq_sum"][:, :], 0.0).then_inc(const, 1)
            pool.memset(A["not_finite"][:, :], 0.0).then_inc(const, 1)
            pool.memset(eps[:, :], EPS).then_inc(const, 1)
            pool.wait_ge(const, 6)
            pool.affine_select(out=A["ident"][:, :], in_=A["ident"][:, :], compare_op=ALU.not_equal, fill=1.0,
                               base=0, pattern=[[-1, P]], channel_multiplier=1).then_inc(const, 1)
            for g in range(P // D):
                pool.affine_select(out=A["fold"][:, :], in_=A["fold"][:, :], compare_op=ALU.not_equal, fill=1.0,
                                   base=-D * g, pattern=[[-1, D]], channel_multiplier=1).then_inc(const, 1)
                pool.wait_ge(const, 8 + g)

            def step(base, slot):
                if (c := at(base, slot, 2, 2, CH)) is not None:
                    add_squares(pool, q_hi[slot], square, A["q_sq_sum"], KT, c, qhi_done, bound_done)

            run_steps(pool, step, CH, 2, first=2, tail=2)

        @block.sync
        def _(sp):
            def step(base, slot):
                if (s := at(base, slot, 0, 2, CH)) is not None:
                    need(sp, x_turned, KT * (s - 1))
                    sp.dma_start(x_in[slot][:, :, :], x_rows[bass.ds(TT * s, TT)].rearrange("t p c -> p t c")) \
                        .then_inc(x_loaded[slot], 16)
                    if isinstance(s, int) and s == 0:
                        sp.dma_start(w[:, :, :], wq.rearrange("(k p) n -> p k n", p=P)).then_inc(w_in, 16)
                        sp.dma_start(bias_raw[:, :], bq.rearrange("(m p) -> p m", p=P),
                                     allow_slow_non_contiguous=True).then_inc(w_in, 16)
                if (c := at(base, slot, 3, 2, CH)) is not None:
                    batch, chunk = base + (slot - 3) // PER, (slot - 3) % PER
                    need(sp, qhi_done, KT * (c + 1))
                    need(sp, qlo_done, KT * (c + 1))
                    for part, q in ((0, q_hi), (1, q_lo)):
                        dst = qT_d[part][bass.ds(C * batch, C), BANK * chunk:BANK * (chunk + 1)]
                        sp.dma_start(dst.rearrange("(m p) n -> p m n", p=P), q[chunk][:, :, :].bitcast(F32)) \
                            .then_inc(q_stored[chunk], 16)

            assert PER == 2
            run_steps(sp, step, CH, 2, first=2, tail=3)
            for i in range(2):
                sp.wait_ge(q_stored[i], 32 * (CH // 2))

        @block.tensor
        def _(pe):
            def step(base, slot):
                par = (slot - 1) % 2
                if (c := at(base, slot, 1, 2, CH)) is not None:
                    need(pe, norm_done, TT * (c + 1))
                    for kt in range(KT):
                        need(pe, xlo_done, KT * (c - 1) + kt + 1)
                        for t in range(TT):
                            mm = pe.transpose(ps[:, kt, P * t:P * (t + 1)], x_in[par][:, t, P * kt:P * (kt + 1)],
                                              A["ident"][:, :])
                        mm.then_inc(x_turned, 1)
                if (c := at(base, slot, 2, 2, CH)) is not None:
                    need(pe, xhi_done, KT * (c + 1))
                    need(pe, xlo_done, KT * (c + 1))
                    if isinstance(c, int) and c == 0:
                        pe.wait_ge(setup, 4)
                    for m in range(KT):
                        need(pe, qlo_done, KT * (c - 1) + m + 1)
                        parts = [(a, b, kt) for kt in range(KT)
                                 for a, b in ((w_hi, xT_hi), (w_lo, xT_hi), (w_hi, xT_lo))]
                        for n, (a, b, kt) in enumerate(parts):
                            mm = pe.matmul(ps[:, 4 + m, :], a[:, kt, P * m:P * (m + 1)], b[slot][:, kt, :],
                                           start=(n == 0), stop=(n == len(parts) - 1))
                        mm.then_inc(q_done, 1)

            pe.wait_ge(const, 11)
            run_steps(pe, step, CH, 2, first=2, tail=2)

        @block.scalar
        def _(act):
            def step(base, slot):
                par = (slot - 1) % 2
                if (c := at(base, slot, 1, 2, CH)) is not None:
                    need(act, q_done, KT * (c - 1))
                    for kt in range(KT):
                        need(act, x_turned, KT * c + kt + 1)
                        act.activation(xT_hi[par][:, kt, :], ps[:, kt, :], ACT.Identity).then_inc(xhi_done, 1)
                if (s := at(base, slot, 0, 2, CH)) is not None:
                    need(act, mv_done, TT * (s + 1))
                    act.activation(std[:, :], meanvar[:, :, 1], ACT.Sqrt, bias=eps[:, 0:1]).then_inc(std_done, 1)
                if (c := at(base, slot, 2, 2, CH)) is not None:
                    need(act, q_stored[slot], 32 * base - 32)
                    if isinstance(c, int) and c == 0:
                        act.wait_ge(setup, 4)
                    need(act, bound_done, 2 * KT * (c - 1))
                    for m in range(KT):
                        need(act, q_done, KT * c + m + 1)
                        act.activation(q_hi[slot][:, m, :], ps[:, 4 + m, :], ACT.Identity, bias=bias[:, m:m + 1]) \
                            .then_inc(qhi_done, 1)

            act.wait_ge(const, 6)
            run_steps(act, step, CH, 2, first=2, tail=2)

        @block.vector
        def _(dve):
            def prepare_weights():
                dve.wait_ge(w_in, 32)
                dve.wait_ge(const, 6)
                dve.tensor_scalar(w[:, :, :], w[:, :, :], SCALE, None, ALU.mult).then_inc(setup, 1)
                dve.tensor_scalar(bias[:, :], bias_raw[:, :], SCALE, None, ALU.mult).then_inc(setup, 1)
                dve.wait_ge(setup, 2)
                dve.tensor_copy(w_hi[:, :, :], w[:, :, :]).then_inc(setup, 1)
                dve.wait_ge(setup, 3)
                dve.tensor_tensor(w_lo[:, :, :], w[:, :, :], w_hi[:, :, :].bitcast(F32), ALU.subtract).then_inc(setup, 1)

            def step(base, slot):
                par = (slot - 1) % 2
                if (c := at(base, slot, 1, 2, CH)) is not None:
                    need(dve, q_done, KT * (c - 1))
                    for kt in range(KT):
                        need(dve, xhi_done, KT * c + kt + 1)
                        dve.tensor_tensor(xT_lo[par][:, kt, :], ps[:, kt, :], xT_hi[par][:, kt, :].bitcast(F32),
                                          ALU.subtract).then_inc(xlo_done, 1)
                if (s := at(base, slot, 0, 2, CH)) is not None:
                    dve.wait_ge(x_loaded[slot], 16 * base + 16)
                    for t in range(TT):
                        dve.bn_stats(stats[:, t, :], x_in[slot][:, t, :]).then_inc(stat_done, 1)
                    need(dve, std_done, s)
                    for t in range(TT):
                        wait_alone(dve, stat_done, TT * s + t + 1, passed)
                        dve.bn_aggr(meanvar[:, t, :], stats[:, t, :]).then_inc(mv_done, 1)
                    dve.wait_ge(std_done, s + 1)
                    dve.reciprocal(rstd[:, :], std[:, :]).then_inc(rstd_done, 1)
                    dve.wait_ge(rstd_done, s + 1)
                    dve.wait_ge(mv_done, TT * s + TT)
                    for t in range(TT):
                        dve.tensor_scalar(x_in[slot][:, t, :], x_in[slot][:, t, :], meanvar[:, t, 0:1],
                                          rstd[:, t:t + 1], ALU.subtract, ALU.mult).then_inc(norm_done, 1)
                    if isinstance(s, int) and s == 0:
                        prepare_weights()
                if (c := at(base, slot, 2, 2, CH)) is not None:
                    need(dve, q_stored[slot], 32 * base - 32)
                    for m in range(KT):
                        dve.wait_ge(qhi_done, KT * c + m + 1)
                        hi = q_hi[slot][:, m, :].bitcast(F32)
                        dve.scalar_tensor_tensor(q_lo[slot][:, m, :], ps[:, 4 + m, :], bias[:, m:m + 1], hi,
                                                 ALU.add, ALU.subtract).then_inc(qlo_done, 1)
                        need(dve, finite_done, KT * c + m)
                        dve.scalar_tensor_tensor(A["not_finite"][:, :], hi, 0.0, A["not_finite"][:, :], ALU.mult,
                                                 ALU.add).then_inc(finite_done, 1)

            run_steps(dve, step, CH, 2, first=2, tail=2)


def project_keys_values(k, A, ctx_in, wk, bk, wv, bv, kT_d, v_d):
    nc, ps = k.nc, k.ps
    B, SK, CK = ctx_in.shape
    C = wk.shape[1]
    KT, MT = CK // P, C // P
    CH = B * SK // BANK
    PER = SK // BANK
    TT = BANK // P
    OUT = MT + TT
    rows = ctx_in.rearrange("b (t p) c -> (b t) p c", p=P)

    with ExitStack() as ctx:
        sb = lambda name, shape, dt=F32: k.sb(ctx, "kv_" + name, shape, dt)
        sem = lambda name: k.sem(ctx, "kv_" + name)
        w = [sb(f"w{i}", [P, KT, C]) for i in range(2)]
        w_hi = [sb(f"w_hi{i}", [P, KT, C], F32R) for i in range(2)]
        w_lo = [sb(f"w_lo{i}", [P, KT, C], F32R) for i in range(2)]
        k_bias = sb("k_bias", [P, MT])
        v_bias = sb("v_bias", [P, C])
        c_in = [sb(f"c_in{i}", [P, TT, CK]) for i in range(2)]
        cT_hi = [sb(f"cT_hi{i}", [P, KT, BANK], F32R) for i in range(2)]
        cT_lo = [sb(f"cT_lo{i}", [P, KT, BANK], F32R) for i in range(2)]
        k_hi = [sb(f"k_hi{i}", [P, MT, BANK], F32R) for i in range(2)]
        k_lo = [sb(f"k_lo{i}", [P, MT, BANK], F32R) for i in range(2)]
        v_out = [sb(f"v_out{i}", [P, HEADS, TT * D]) for i in range(2)]
        ends = sb("ends", [P, 4])
        square = sb("square", [P, BANK])
        one_row = sb("one_row", [1, P])
        found = sb("found", [1, 4])
        pick = sb("pick", [1, 4])

        w_in = sem("w_in")
        setup = sem("setup")
        c_loaded = [sem(f"c_loaded{i}") for i in range(2)]
        c_turned = sem("c_turned")
        chi_done = sem("chi_done")
        clo_done = sem("clo_done")
        kv_done = sem("kv_done")
        khi_done = sem("khi_done")
        klo_done = sem("klo_done")
        v_done = sem("v_done")
        bound_done = sem("bound_done")
        finite_done = sem("finite_done")
        stored = [sem(f"stored{i}") for i in range(2)]
        path = sem("path")
        path_pe = sem("path_pe")
        block = ctx.enter_context(nc.Block())

        @block.gpsimd
        def _(pool):
            def step(base, slot):
                if (c := at(base, slot, 1, 2, CH)) is not None:
                    add_squares(pool, k_hi[(slot - 1) % 2], square, A["k_sq_sum"], MT, c, khi_done,
                                        bound_done)

            run_steps(pool, step, CH, 2, first=2, tail=1)

        @block.sync
        def _(sp):
            def step(base, slot):
                par = slot % 2
                if (s := at(base, slot, 0, PER, CH)) is not None:
                    need(sp, c_turned, KT * (s - 1))
                    sp.dma_start(c_in[par][:, :, :], rows[bass.ds(TT * s, TT)].rearrange("t p c -> p t c")) \
                        .then_inc(c_loaded[par], 16)
                    if isinstance(s, int) and s == 0:
                        for i, src in enumerate((wk, wv)):
                            sp.dma_start(w[i][:, :, :], src.rearrange("(k p) n -> p k n", p=P)).then_inc(w_in, 16)
                        sp.dma_start(k_bias[:, :], bk.rearrange("(m p) -> p m", p=P),
                                     allow_slow_non_contiguous=True).then_inc(w_in, 16)
                        sp.dma_start(v_bias[:, :], bv.partition_broadcast(P)).then_inc(w_in, 16)
                if (c := at(base, slot, 2, PER, CH)) is not None:
                    batch, chunk = base + (slot - 2) // PER, (slot - 2) % PER
                    par = chunk % 2
                    need(sp, khi_done, MT * (c + 1))
                    need(sp, klo_done, MT * (c + 1))
                    for part, kk in ((0, k_hi), (1, k_lo)):
                        dst = kT_d[part][bass.ds(C * batch, C), BANK * chunk:BANK * (chunk + 1)]
                        sp.dma_start(dst.rearrange("(m p) n -> p m n", p=P), kk[par][:, :, :].bitcast(F32)) \
                            .then_inc(stored[par], 16)
                    need(sp, v_done, TT * (c + 1))
                    dst = v_d[bass.ds(HEADS * batch, HEADS), :, TT * D * chunk:TT * D * (chunk + 1)]
                    sp.dma_start(dst.rearrange("h p n -> p h n"), v_out[par][:, :, :]).then_inc(stored[par], 16)

            run_steps(sp, step, CH, PER, first=1, tail=2)
            for i in range(2):
                sp.wait_ge(stored[i], 48 * (CH // 2))

        @block.tensor
        def _(pe):
            def step(base, slot):
                if (s := at(base, slot, 0, 2, CH)) is not None:
                    pe.wait_ge(c_loaded[slot], 16 * base + 16)
                    for kt in range(KT):
                        need(pe, clo_done, KT * (s - 1) + kt + 1)
                        for t in range(TT):
                            mm = pe.transpose(ps[:, kt, P * t:P * (t + 1)], c_in[slot][:, t, P * kt:P * (kt + 1)],
                                              A["ident"][:, :])
                        mm.then_inc(c_turned, 1)
                if (c := at(base, slot, 1, 2, CH)) is not None:
                    par = (slot - 1) % 2
                    need(pe, chi_done, KT * (c + 1))
                    need(pe, clo_done, KT * (c + 1))
                    if isinstance(c, int) and c == 0:
                        pe.wait_ge(setup, 4)
                    for m in range(MT):
                        need(pe, v_done, TT * (c - 1) + m + 1)
                        parts = [(a, b, kt) for kt in range(KT)
                                 for a, b in ((w_hi, cT_hi), (w_lo, cT_hi), (w_hi, cT_lo))]
                        for n, (a, b, kt) in enumerate(parts):
                            mm = pe.matmul(ps[:, 4 + m, :], a[0][:, kt, P * m:P * (m + 1)], b[par][:, kt, :],
                                           start=(n == 0), stop=(n == len(parts) - 1))
                        mm.then_inc(kv_done, 1)
                    for t in range(TT):
                        need(pe, klo_done, MT * c + t + 1)
                        parts = [(a, b, kt) for kt in range(KT)
                                 for a, b in ((cT_hi, w_hi), (cT_hi, w_lo), (cT_lo, w_hi))]
                        for n, (a, b, kt) in enumerate(parts):
                            mm = pe.matmul(ps[:, 4 + t, :], a[par][:, kt, P * t:P * (t + 1)], b[1][:, kt, :],
                                           start=(n == 0), stop=(n == len(parts) - 1))
                        mm.then_inc(kv_done, 1)

            run_steps(pe, step, CH, 2, first=2, tail=1)
            pe.wait_ge(path, 5)
            for i in range(3):
                mm = pe.transpose(ps[0:1, 0, P * i:P * (i + 1)], ends[:, i:i + 1], A["ident"][:, :])
            mm.then_inc(path_pe, 1)
            pe.wait_ge(path, 10)
            pe.matmul(ps[:, 1, 0:1], one_row[:, :], pick[:, 2:3], start=True, stop=True).then_inc(path_pe, 1)

        @block.scalar
        def _(act):
            def step(base, slot):
                if (s := at(base, slot, 0, 2, CH)) is not None:
                    need(act, kv_done, OUT * (s - 1))
                    for kt in range(KT):
                        need(act, c_turned, KT * s + kt + 1)
                        act.activation(cT_hi[slot][:, kt, :], ps[:, kt, :], ACT.Identity).then_inc(chi_done, 1)
                if (c := at(base, slot, 1, 2, CH)) is not None:
                    par = (slot - 1) % 2
                    need(act, stored[par], 48 * (base + (slot - 1) // 2))
                    need(act, bound_done, 2 * MT * (c - 1))
                    if isinstance(c, int) and c == 0:
                        act.wait_ge(w_in, 64)
                    for m in range(MT):
                        need(act, kv_done, OUT * c + m + 1)
                        act.activation(k_hi[par][:, m, :], ps[:, 4 + m, :], ACT.Identity, bias=k_bias[:, m:m + 1]) \
                            .then_inc(khi_done, 1)

            run_steps(act, step, CH, 2, first=2, tail=1)

        @block.vector
        def _(dve):
            def prepare_weights():
                dve.wait_ge(w_in, 64)
                for i in range(2):
                    dve.tensor_copy(w_hi[i][:, :, :], w[i][:, :, :]).then_inc(setup, 1)
                for i in range(2):
                    dve.wait_ge(setup, i + 1)
                    dve.tensor_tensor(w_lo[i][:, :, :], w[i][:, :, :], w_hi[i][:, :, :].bitcast(F32),
                                      ALU.subtract).then_inc(setup, 1)

            def step(base, slot):
                if (s := at(base, slot, 0, 2, CH)) is not None:
                    need(dve, kv_done, OUT * (s - 1))
                    for kt in range(KT):
                        need(dve, chi_done, KT * s + kt + 1)
                        dve.tensor_tensor(cT_lo[slot][:, kt, :], ps[:, kt, :], cT_hi[slot][:, kt, :].bitcast(F32),
                                          ALU.subtract).then_inc(clo_done, 1)
                    if isinstance(s, int) and s == 0:
                        prepare_weights()
                if (c := at(base, slot, 1, 2, CH)) is not None:
                    par = (slot - 1) % 2
                    need(dve, stored[par], 48 * (base + (slot - 1) // 2))
                    for m in range(MT):
                        dve.wait_ge(khi_done, MT * c + m + 1)
                        hi = k_hi[par][:, m, :].bitcast(F32)
                        dve.scalar_tensor_tensor(k_lo[par][:, m, :], ps[:, 4 + m, :], k_bias[:, m:m + 1], hi,
                                                 ALU.add, ALU.subtract).then_inc(klo_done, 1)
                        need(dve, finite_done, MT * c + m)
                        dve.scalar_tensor_tensor(A["not_finite"][:, :], hi, 0.0, A["not_finite"][:, :], ALU.mult,
                                                 ALU.add).then_inc(finite_done, 1)
                    for t in range(TT):
                        dve.wait_ge(kv_done, OUT * c + MT + t + 1)
                        dve.tensor_tensor(v_out[par][:, :, D * t:D * (t + 1)],
                                          ps[:, 4 + t, :].rearrange("p (h d) -> p h d", d=D),
                                          v_bias[:, :].rearrange("p (h d) -> p h d", d=D), ALU.add) \
                            .then_inc(v_done, 1)

            run_steps(dve, step, CH, 2, first=2, tail=1)
            dve.wait_ge(finite_done, MT * CH)
            dve.wait_ge(bound_done, 2 * MT * CH)
            dve.tensor_reduce(ends[:, 0:1], A["q_sq_sum"][:, :], AX_X, ALU.max).then_inc(path, 1)
            dve.tensor_reduce(ends[:, 1:2], A["k_sq_sum"][:, :], AX_X, ALU.max).then_inc(path, 1)
            dve.tensor_reduce(ends[:, 3:4], A["not_finite"][:, :], AX_X, ALU.add).then_inc(path, 1)
            dve.memset(one_row[:, :], 1.0).then_inc(path, 1)
            dve.wait_ge(path, 4)
            dve.tensor_tensor(ends[:, 2:3], ends[:, 3:4], ends[:, 3:4], ALU.not_equal).then_inc(path, 1)
            dve.wait_ge(path_pe, 1)
            dve.tensor_reduce(found[:, 0:3], ps[0:1, 0, 0:3 * P].rearrange("p (i n) -> p i n", n=P), AX_X,
                              ALU.max).then_inc(path, 1)
            dve.wait_ge(path, 6)
            dve.tensor_tensor(pick[:, 0:1], found[:, 0:1], found[:, 1:2], ALU.mult).then_inc(path, 1)
            dve.wait_ge(path, 7)
            dve.tensor_scalar(pick[:, 1:2], pick[:, 0:1], (0.99 * CLAMP / D) ** 2, None, ALU.is_gt).then_inc(path, 1)
            dve.tensor_scalar(pick[:, 2:3], found[:, 2:3], -CLAMP, CLAMP, ALU.mult, ALU.add).then_inc(path, 1)
            dve.wait_ge(path, 9)
            dve.tensor_tensor(A["clip_path"][:, :], pick[:, 1:2], found[:, 2:3], ALU.max).then_inc(path, 1)
            dve.wait_ge(path_pe, 2)
            dve.tensor_copy(A["clip_high"][:, :], ps[:, 1, 0:1]).then_inc(path, 1)
            dve.wait_ge(path, 11)
            dve.tensor_scalar(A["clip_low"][:, :], A["clip_high"][:, :], -1.0, None, ALU.mult).then_inc(path, 1)


def attend(k, A, shape, qT_d, kT_d, v_d, oT_d, sum_d, w1_raw, fc1_q, fc1_scales, w1_loaded):
    nc, ps = k.nc, k.ps
    B, SQ, SK = shape
    N_HEADS = B * HEADS
    HALVES = SQ // BANK
    QT = BANK // P
    PER_HEAD = HALVES * QT
    UNROLL = 2 * PER_HEAD
    BODY = UNROLL // QT
    STEPS = N_HEADS * PER_HEAD
    KVT = SK // P
    ROW, KEYS, PV, PART, FOLD, GATHER = 4, 5, 6, 9, 12, 14
    GP_ADDS = 5
    PARTS = 3 * D
    assert SK == 4 * BANK and HALVES == 2 and KVT == 16

    def lagged(base, slot, lag):
        if at(base, slot, lag, UNROLL, STEPS) is None:
            return None, None
        return BODY * base + (slot - lag) // QT, (slot - lag) % QT

    with ExitStack() as ctx:
        sb = lambda name, shape, dt=F32: k.sb(ctx, "at_" + name, shape, dt)
        sem = lambda name: k.sem(ctx, "at_" + name)
        k_stack = [sb(f"k_stack{i}", [P, SK], F32R) for i in range(2)]
        q_stack = [sb(f"q_stack{i}", [P, SQ], F32R) for i in range(2)]
        v_head = [sb(f"v_head{i}", [P, KVT, D]) for i in range(2)]
        probT = [sb(f"probT{i}", [P, KVT, BANK]) for i in range(2)]
        gp_sum = [sb(f"gp_sum{i}", [P, 2, BANK]) for i in range(2)]
        total = sb("total", [P, 2, BANK])
        half_max = sb("half_max", [P, BODY * QT, 2])
        row_max = sb("row_max", [P, QT])
        neg_hi = sb("neg_hi", [P, QT, 2], F32R)
        partial = sb("partial", [P, BANK])
        result = [sb(f"result{i}", [P, BANK]) for i in range(2)]
        ident_r = sb("ident_r", [P, P], F32R)
        ones = sb("ones", [P, D])
        ones_wide = sb("ones_wide", [P, BANK])
        clipped = sb("clipped", [P, 2 * BANK])
        wide = sb("wide", [P, 2, QT, P], F32R)
        neg_rows = [sb(f"neg_rows{i}", [P, BANK]) for i in range(2)]
        shifted = [sb(f"shifted{i}", [P, BANK]) for i in range(2)]

        const = sem("const")
        qk_loaded = [sem(f"qk_loaded{i}") for i in range(2)]
        v_loaded = [sem(f"v_loaded{i}") for i in range(2)]
        score_done = sem("score_done")
        max_done = sem("max_done")
        split_done = sem("split_done")
        row_turned = sem("row_turned")
        row_copied = sem("row_copied")
        tile_done = sem("tile_done")
        clip_done = sem("clip_done")
        shift_done = sem("shift_done")
        exp_done = sem("exp_done")
        gp_added = sem("gp_added")
        total_done = sem("total_done")
        pv_done = sem("pv_done")
        partial_done = sem("partial_done")
        fold_done = sem("fold_done")
        gather_done = sem("gather_done")
        stored = [sem(f"stored{i}") for i in range(2)]
        block = ctx.enter_context(nc.Block())

        def by_path(eng, steps):
            clipping = eng.value_load(A["clip_path"][0:1, 0:1], min_val=0, max_val=1)
            with eng.If(clipping > 0):
                steps(eng, True)
            with eng.Else():
                steps(eng, False)

        @block.gpsimd
        def _(pool):
            def step(base, lane):
                unit = BODY * base + lane
                pairs = probT[lane % 2]
                need(pool, fold_done, unit - 1)
                pool.wait_ge(exp_done, KVT * unit + 4)
                pool.tensor_tensor(gp_sum[lane % 2][:, :, :], pairs[:, 0:2, :], pairs[:, 2:4, :], ALU.add) \
                    .then_inc(gp_added, 1)
                for i in range(1, GP_ADDS):
                    pool.wait_ge(exp_done, KVT * unit + 2 * i + 4)
                    pool.wait_ge(gp_added, GP_ADDS * unit + i)
                    pool.tensor_tensor(gp_sum[lane % 2][:, :, :], gp_sum[lane % 2][:, :, :],
                                       pairs[:, 2 * i + 2:2 * i + 4, :], ALU.add).then_inc(gp_added, 1)

            pool.memset(ones[:, :], 1.0).then_inc(const, 1)
            pool.memset(ones_wide[:, :], 1.0).then_inc(const, 1)
            run_steps(pool, step, STEPS // QT, BODY, first=1)

        @block.sync
        def _(sp):
            def step(base, slot):
                if (n := at(base, slot, 0, 2, N_HEADS)) is not None:
                    need(sp, tile_done, HALVES * KVT * (n - 1))
                    r = bass.ds(D * n, D)
                    for g in range(3):
                        rows = slice(D * g, D * (g + 1))
                        sp.dma_start(q_stack[slot][rows, :].bitcast(F32), qT_d[g // 2][r, :]) \
                            .then_inc(qk_loaded[slot], 16)
                        sp.dma_start(k_stack[slot][rows, :].bitcast(F32), kT_d[g % 2][r, :]) \
                            .then_inc(qk_loaded[slot], 16)
                    need(sp, pv_done, HALVES * (n - 1))
                    sp.dma_start(v_head[slot][:, :, :].rearrange("p t d -> p (t d)"),
                                 v_d[bass.ds(n, 1)].rearrange("h p n -> (h p) n")).then_inc(v_loaded[slot], 16)
                if (n := at(base, slot, 2, 2, N_HEADS)) is not None:
                    for half in range(HALVES):
                        sp.wait_ge(gather_done, HALVES * n + half + 1)
                        cols = slice(BANK * half, BANK * (half + 1))
                        sp.dma_start(oT_d[bass.ds(D * n, D), cols], result[half][0:D, :]).then_inc(stored[half], 16)
                        for i in range(3):
                            sp.dma_start(sum_d[i][bass.ds(n, 1), cols], result[half][D * (i + 1):D * (i + 1) + 1, :]) \
                                .then_inc(stored[half], 16)

            run_steps(sp, step, N_HEADS, 2, first=2, tail=2)
            for half in range(HALVES):
                sp.wait_ge(stored[half], 64 * N_HEADS)

        def pe_steps(pe, clipping):
            def scores(base, slot, n):
                s = at(base, slot, 0, UNROLL, STEPS)
                if s is None:
                    return
                par = slot // PER_HEAD
                rows = slice(P * (slot % PER_HEAD), P * (slot % PER_HEAD + 1))
                if n == 0 and slot % PER_HEAD == 0:
                    pe.wait_ge(qk_loaded[par], 96 * base + 96)
                if n % 2 == 0:
                    need(pe, max_done, 2 * (s - 1) + n // 2 + 1)
                mm = pe.matmul(ps[:, n, :], q_stack[par][0:PARTS, rows],
                               k_stack[par][0:PARTS, BANK * n:BANK * (n + 1)], start=True, stop=True)
                if n % 2:
                    mm.then_inc(score_done, 1)

            def keys(base, slot, i):
                unit, r = lagged(base, slot, KEYS)
                if unit is None:
                    return
                lane = (slot - KEYS) // QT % BODY
                kv = 4 * r + i
                par, rows = lane // HALVES, PARTS if clipping else PARTS + 2
                if kv == 0:
                    pe.wait_ge(row_copied, unit + 1)
                need(pe, exp_done, KVT * unit + kv - 1)
                q = BANK * (lane % HALVES)
                pe.matmul(ps[:, 4 + kv % 2, :],
                          k_stack[par][0:rows, P * kv:P * (kv + 1)], q_stack[par][0:rows, q:q + BANK],
                          start=True, stop=True).then_inc(tile_done, 1)

            def turn_maxima(base, slot):
                if (slot - ROW) % QT or at(base, slot, ROW, UNROLL, STEPS) is None:
                    return
                unit = BODY * base + (slot - ROW) // QT
                pe.wait_ge(split_done, (5 if clipping else 3) * (unit + 1))
                need(pe, gather_done, unit - (FOLD - ROW) // QT)
                for t in range(QT):
                    cols = slice(P * t, P * (t + 1))
                    if clipping:
                        for part in range(2):
                            mm = pe.matmul(ps[:, 7, cols], wide[:, part, t, :], ident_r[:, :],
                                           start=(part == 0), stop=(part == 1))
                    else:
                        mm = pe.matmul(ps[0:2, 7, cols], neg_hi[:, t, :], ident_r[:, :],
                                       start=True, stop=True)
                mm.then_inc(row_turned, 1)

            def values(base, slot):
                unit, r = lagged(base, slot, PV)
                if unit is None:
                    return
                lane = (slot - PV) // QT % BODY
                head = lane // HALVES
                pe.wait_ge(exp_done, KVT * unit + 4 * r + 4)
                if r == 0:
                    pe.wait_ge(v_loaded[head], 16 * (base if slot >= PV else base - 1) + 16)
                    need(pe, partial_done, unit)
                for g in range(4):
                    mm = pe.matmul(ps[D * g:D * (g + 1), 6, :], v_head[head][:, 4 * r + g, :],
                                   probT[lane % 2][:, 4 * r + g, :], start=(r == 0), stop=(r == QT - 1))
                if r == QT - 1:
                    mm.then_inc(pv_done, 1)

            def fold(base, slot):
                unit, r = lagged(base, slot, FOLD)
                if unit is None or r:
                    return
                lane = (slot - FOLD) // QT % BODY
                if at(base, slot, ROW, UNROLL, STEPS) is not None:
                    pe.wait_ge(row_copied, unit + (FOLD - ROW) // QT + 1)
                need(pe, gather_done, unit)
                pe.wait_ge(partial_done, unit + 1)
                pe.wait_ge(total_done, 2 * unit + 2)
                for g, (a, b) in enumerate(((A["fold"], partial[:, :]), (ones, total[:, 0, :]), (ones, total[:, 1, :]),
                                            (ones, gp_sum[lane % 2][:, 1, :]))):
                    mm = pe.matmul(ps[D * g:D * (g + 1), 7, :], a[:, :], b, start=True, stop=True)
                mm.then_inc(fold_done, 1)

            def step(base, slot):
                scores(base, slot, 0)
                keys(base, slot, 0)
                scores(base, slot, 1)
                keys(base, slot, 1)
                values(base, slot)
                turn_maxima(base, slot)
                keys(base, slot, 2)
                scores(base, slot, 2)
                keys(base, slot, 3)
                scores(base, slot, 3)
                fold(base, slot)

            run_steps(pe, step, STEPS, UNROLL, first=1, tail=GATHER)

        @block.tensor
        def _(pe):
            pe.wait_ge(const, 7)
            by_path(pe, pe_steps)

        def act_steps(act, clipping):
            def exps(base, slot, i):
                unit, r = lagged(base, slot, KEYS)
                if unit is None:
                    return
                lane = (slot - KEYS) // QT % BODY
                kv = 4 * r + i
                if kv == 0:
                    need(act, pv_done, unit - 1)
                    need(act, gp_added, GP_ADDS * (unit - 1))
                    need(act, total_done, 2 * (unit - 1) - 1)
                if clipping:
                    act.wait_ge(shift_done, KVT * unit + kv + 1)
                    src = shifted[kv % 2][:, :]
                else:
                    act.wait_ge(tile_done, KVT * unit + kv + 1)
                    src = ps[:, 4 + kv % 2, :]
                act.activation(probT[lane % 2][:, kv, :], src, ACT.Exp).then_inc(exp_done, 1)

            def copy_maxima(base, slot):
                if (slot - ROW) % QT or at(base, slot, ROW, UNROLL, STEPS) is None:
                    return
                unit, lane = BODY * base + (slot - ROW) // QT, (slot - ROW) // QT
                act.wait_ge(row_turned, unit + 1)
                if clipping:
                    need(act, shift_done, KVT * (unit - 1))
                    act.copy(neg_rows[lane % 2][:, :], ps[:, 7, :]).then_inc(row_copied, 1)
                else:
                    q = BANK * (lane % HALVES)
                    act.activation(q_stack[lane // HALVES][PARTS:PARTS + 2, q:q + BANK],
                                   ps[0:2, 7, :], ACT.Identity).then_inc(row_copied, 1)

            def step(base, slot):
                exps(base, slot, 0)
                exps(base, slot, 1)
                if (slot - PART) % QT == 0 and at(base, slot, PART, UNROLL, STEPS) is not None:
                    unit = BODY * base + (slot - PART) // QT
                    act.wait_ge(pv_done, unit + 1)
                    need(act, fold_done, unit)
                    act.copy(partial[:, :], ps[:, 6, :]).then_inc(partial_done, 1)
                copy_maxima(base, slot)
                if (slot - GATHER) % QT == 0 and at(base, slot, GATHER, UNROLL, STEPS) is not None:
                    unit, lane = BODY * base + (slot - GATHER) // QT, (slot - GATHER) // QT
                    act.wait_ge(fold_done, unit + 1)
                    need(act, stored[lane % 2], 64 * (2 * base + lane // HALVES))
                    act.copy(result[lane % 2][:, :], ps[:, 7, :]).then_inc(gather_done, 1)
                exps(base, slot, 2)
                exps(base, slot, 3)

            run_steps(act, step, STEPS, UNROLL, first=1, tail=GATHER)

        @block.scalar
        def _(act):
            act.dma_start(w1_raw[1][:, :, :], fc1_q.rearrange("(k p) n -> p k n", p=P)).then_inc(w1_loaded, 16)
            act.dma_start(w1_raw[0][:, :], fc1_scales.rearrange("k n -> (k n)").partition_broadcast(P)) \
                .then_inc(w1_loaded, 16)
            by_path(act, act_steps)

        def dve_steps(dve, clipping):
            def maxima(slot, s, half):
                dve.wait_ge(score_done, 2 * s + half + 1)
                dst = half_max[:, slot, half:half + 1]
                src = ps[:, 2 * half:2 * half + 2, :].rearrange("p b n -> p (b n)")
                if clipping:
                    need(dve, max_done, 2 * s + half)
                    dve.tensor_scalar(clipped[:, :], src, A["clip_high"][:, 0:1], None, ALU.min, ALU.max,
                                      accum_out=dst).then_inc(max_done, 1)
                else:
                    dve.tensor_reduce(dst, src, AX_X, ALU.max).then_inc(max_done, 1)

            def split_maxima(base, slot):
                if (slot - ROW) % QT or at(base, slot, ROW, UNROLL, STEPS) is None:
                    return
                unit, first = BODY * base + (slot - ROW) // QT, (slot - ROW) % UNROLL
                n = 5 if clipping else 3
                pair = half_max[:, first:first + QT, :]
                dve.wait_ge(max_done, 2 * QT * (unit + 1))
                need(dve, split_done, n * unit)
                if clipping:
                    dve.scalar_tensor_tensor(row_max[:, :], pair[:, :, 0], A["clip_low"][:, 0:1], pair[:, :, 1],
                                             ALU.max, ALU.max).then_inc(split_done, 1)
                else:
                    dve.tensor_tensor(row_max[:, :], pair[:, :, 0], pair[:, :, 1], ALU.max).then_inc(split_done, 1)
                dve.wait_ge(split_done, n * unit + 1)
                need(dve, row_turned, unit)
                dve.tensor_scalar(neg_hi[:, :, 0], row_max[:, :], -1.0, None, ALU.mult).then_inc(split_done, 1)
                dve.wait_ge(split_done, n * unit + 2)
                dve.scalar_tensor_tensor(neg_hi[:, :, 1], row_max[:, :], -1.0, neg_hi[:, :, 0].bitcast(F32),
                                         ALU.mult, ALU.subtract).then_inc(split_done, 1)
                if clipping:
                    dve.wait_ge(split_done, n * unit + 3)
                    for part in range(2):
                        dve.tensor_copy(wide[:, part, :, :], neg_hi[:, :, part:part + 1].bitcast(F32)
                                        .to_broadcast([P, QT, P])).then_inc(split_done, 1)

            def shift(base, slot, i):
                unit, r = lagged(base, slot, KEYS)
                if unit is None or not clipping:
                    return
                lane = (slot - KEYS) // QT % BODY
                kv = 4 * r + i
                n = KVT * unit + kv
                dve.wait_ge(tile_done, n + 1)
                need(dve, exp_done, n - 1)
                dve.tensor_scalar(shifted[kv % 2][:, :], ps[:, 4 + kv % 2, :],
                                  A["clip_high"][:, 0:1], A["clip_low"][:, 0:1], ALU.min, ALU.max) \
                    .then_inc(clip_done, 1)
                dve.wait_ge(clip_done, n + 1)
                dve.wait_ge(row_copied, unit + 1)
                dve.tensor_tensor(shifted[kv % 2][:, :], shifted[kv % 2][:, :], neg_rows[lane % 2][:, :],
                                  ALU.add).then_inc(shift_done, 1)

            def totals(base, slot):
                if (slot - PART) % QT == 0 and at(base, slot, PART, UNROLL, STEPS) is not None:
                    unit, lane = BODY * base + (slot - PART) // QT, (slot - PART) // QT
                    last = probT[lane % 2][:, KVT - 4:KVT, :]
                    dve.wait_ge(exp_done, KVT * unit + KVT)
                    need(dve, fold_done, unit)
                    dve.tensor_tensor(total[:, :, :], last[:, 0:2, :], last[:, 2:4, :], ALU.add) \
                        .then_inc(total_done, 1)
                if (slot - FOLD + 1) % QT == 0 and at(base, slot, FOLD - 1, UNROLL, STEPS) is not None:
                    unit, lane = BODY * base + (slot - FOLD + 1) // QT, (slot - FOLD + 1) // QT
                    dve.wait_ge(gp_added, GP_ADDS * unit + GP_ADDS)
                    dve.wait_ge(total_done, 2 * unit + 1)
                    dve.tensor_tensor(total[:, 0, :], total[:, 0, :], gp_sum[lane % 2][:, 0, :], ALU.add) \
                        .then_inc(total_done, 1)

            def step(base, slot):
                s = at(base, slot, 0, UNROLL, STEPS)
                split_maxima(base, slot)
                if s is not None:
                    maxima(slot, s, 0)
                shift(base, slot, 0)
                shift(base, slot, 1)
                totals(base, slot)
                if s is not None:
                    maxima(slot, s, 1)
                shift(base, slot, 2)
                shift(base, slot, 3)

            run_steps(dve, step, STEPS, UNROLL, first=1, tail=GATHER)

        @block.vector
        def _(dve):
            dve.tensor_copy(ident_r[:, :], A["ident"][:, :]).then_inc(const, 1)
            dve.wait_ge(const, 3)
            for stack in k_stack:
                for n in range(SK // BANK // 2):
                    dve.tensor_copy(stack[PARTS:PARTS + 2, 2 * BANK * n:2 * BANK * (n + 1)].rearrange(
                        "p (a n) -> p a n", a=2), ones_wide[PARTS:PARTS + 2, :].unsqueeze(1)
                        .to_broadcast([2, 2, BANK])).then_inc(const, 1)
            by_path(dve, dve_steps)


def project_out(k, A, x, oT_d, sum_d, inv_d, wo, bo, g_attn, g_ffn, x1_d, raws, weights, fc2_q, fc2_scales, w1_loaded):
    nc, ps = k.nc, k.ps
    B, SQ, C = x.shape
    KT, TT = C // P, BANK // P
    CH = B * SQ // BANK
    x_rows = x.rearrange("b (t p) c -> (b t) p c", p=P)

    with ExitStack() as ctx:
        sb = lambda name, shape, dt=F32: k.sb(ctx, "po_" + name, shape, dt)
        sem = lambda name: k.sem(ctx, "po_" + name)
        w_hi = sb("w_hi", [P, KT, C], F32R)
        w_lo = sb("w_lo", [P, KT, C], F32R)
        gates = sb("gates", [P, 2])
        tanhs = sb("tanhs", [P, 2])
        bias = sb("bias", [P, C])
        with ExitStack() as first:
            oT_in = [k.sb(first, f"po_oT_in{i}", [P, KT, BANK]) for i in range(2)]
        oT_lo = [sb(f"oT_lo{i}", [P, KT, BANK], F32R) for i in range(2)]
        inverse = sb("inverse", [P, KT, BANK])
        x_in = [sb(f"x_in{i}", [P, TT, C]) for i in range(2)]
        weight = [sb(f"weight{i}", [P, BANK]) for i in range(2)]
        oT_hi = [sb(f"oT_hi{i}", [P, KT, BANK], F32R) for i in range(2)]
        eps = sb("eps", [P, 1])
        stats = sb("stats", [P, TT, 6])
        meanvar = sb("meanvar", [P, TT, 2])
        mv_all = sb("mv_all", [P, CH * TT, 2])
        small = weight[0][:, 0:6 * CH * TT].rearrange("p (i n) -> p i n", i=6)

        w_in = sem("w_in")
        w2_loaded = sem("w2_loaded")
        sums_in = sem("sums_in")
        inverted = sem("inverted")
        div_done = sem("div_done")
        weight_done = sem("weight_done")
        whi_done = sem("whi_done")
        wlo_done = sem("wlo_done")
        tanh_done = sem("tanh_done")
        setup = sem("setup")
        passed = sem("passed")
        o_loaded = [sem(f"o_loaded{i}") for i in range(2)]
        x_loaded = [sem(f"x_loaded{i}") for i in range(2)]
        ohi_done = sem("ohi_done")
        olo_done = sem("olo_done")
        out_done = sem("out_done")
        biased = sem("biased")
        x1_done = sem("x1_done")
        stat_done = sem("stat_done")
        mv_done = sem("mv_done")
        kept = sem("kept")
        x1_stored = [sem(f"x1_stored{i}") for i in range(2)]
        end = sem("end")
        root = sem("root")
        block = ctx.enter_context(nc.Block())
        w_stage = x_in[1]
        sums = x_in[0]
        assert B * HEADS * SQ == P * BANK and C == BANK

        flat = [[w[part][:, :, :].rearrange("p k n -> p (k n)") for part in range(2)] for w in weights]
        scales = [raw[0] for raw in raws]
        codes = [raw[1][:, :, :].rearrange("p k n -> p (k n)") for raw in raws]
        PIECES = flat[0][0].shape[1] // BANK
        PER_STEP = 2 * PIECES // CH
        assert PER_STEP == TT and flat[1][0].shape[1] // BANK == PIECES and PIECES == PER_STEP * CH // 2

        def piece(c, j):
            if isinstance(c, int) and c < CH // 2:
                n = PER_STEP * c + j
                return 0, slice(BANK * n, BANK * (n + 1))
            n = PER_STEP * c + j - PIECES
            return 1, slice(BANK * n, BANK * (n + 1)) if isinstance(n, int) else bass.ds(BANK * n, BANK)

        @block.gpsimd
        def _(pool):
            def step(base, slot):
                if (s := at(base, slot, 0, 2, CH)) is not None:
                    pool.wait_ge(o_loaded[slot], 80 * base + 80)
                    for kt in range(KT):
                        pool.tensor_tensor(oT_in[slot][:, kt, :], oT_in[slot][:, kt, :], inverse[:, kt, :],
                                           ALU.mult).then_inc(div_done, 1)
                if (c := at(base, slot, 1, 2, CH)) is not None:
                    par, uses = (slot - 1) % 2, base + (slot - 1) // 2
                    if isinstance(c, int) and c == 0:
                        pool.wait_ge(setup, 3)
                    pool.wait_ge(x_loaded[par], 16 * uses + 16 + 16 * par)
                    pool.tensor_tensor(x_in[par][:, :, :], x_in[par][:, :, :],
                                       bias[:, :].unsqueeze(1).to_broadcast([P, TT, C]), ALU.add).then_inc(biased, 1)

            run_steps(pool, step, CH, 2, first=1, tail=1)

        @block.sync
        def _(sp):
            def load_outputs(base, slot, s):
                need(sp, out_done, TT * (s - 1))
                sp.dma_start(oT_in[slot][:, :, :], oT_d[bass.ds(C * base, C), BANK * slot:BANK * (slot + 1)]
                             .rearrange("(k p) n -> p k n", p=P)).then_inc(o_loaded[slot], 16)

            def step(base, slot):
                if (s := at(base, slot, 0, 2, CH)) is not None:
                    if not isinstance(s, int) or s >= 2:
                        load_outputs(base, slot, s)
                    need(sp, div_done, KT * s)
                    for g in range(P // D):
                        heads = inv_d[bass.ds(HEADS * base, HEADS), BANK * slot:BANK * (slot + 1)]
                        sp.dma_start(inverse[D * g:D * (g + 1), :, :], heads.rearrange("(k g) n -> g k n", g=P // D)[g]
                                     .partition_broadcast(D)).then_inc(o_loaded[slot], 16)
                    if isinstance(s, int) and s < CH // 2:
                        q = slice(PER_STEP * s, PER_STEP * (s + 1))
                        need(sp, w2_loaded, 32 * s)
                        sp.dma_start(raws[1][1][:, q, :], fc2_q.rearrange("(k p) n -> p k n", p=P)[:, q, :]) \
                            .then_inc(w2_loaded, 16)
                        sp.dma_start(raws[1][0][:, BANK * q.start:BANK * q.stop], fc2_scales[q, :]
                                     .rearrange("k n -> (k n)").partition_broadcast(P)).then_inc(w2_loaded, 16)
                if (c := at(base, slot, 2, 2, CH)) is not None:
                    sp.wait_ge(x1_done, TT * c + TT)
                    sp.dma_start(x1_d[bass.ds(TT * c, TT)].rearrange("t p c -> p t c"), x_in[slot][:, :, :]) \
                        .then_inc(x1_stored[slot], 16)
                if (c := at(base, slot, 1, 2, CH)) is not None:
                    par, uses = (slot - 1) % 2, base + (slot - 1) // 2
                    need(sp, setup, 3 * par)
                    need(sp, x1_stored[par], 16 * uses)
                    need(sp, stat_done, TT * (c - 1))
                    sp.dma_start(x_in[par][:, :, :], x_rows[bass.ds(TT * c, TT)].rearrange("t p c -> p t c")) \
                        .then_inc(x_loaded[par], 16)

            for i in range(3):
                sp.dma_start(sums[:, i, :], sum_d[i].rearrange("h (a n) -> (h a) n", n=BANK)).then_inc(sums_in, 16)
            sp.dma_start(w_stage[:, :, :], wo.rearrange("(k p) n -> p k n", p=P)).then_inc(x_loaded[1], 16)
            sp.dma_start(gates[:, 0:1], g_attn.partition_broadcast(P)).then_inc(w_in, 16)
            sp.dma_start(gates[:, 1:2], g_ffn.partition_broadcast(P)).then_inc(w_in, 16)
            sp.dma_start(bias[:, :], bo.partition_broadcast(P)).then_inc(w_in, 16)
            for slot in range(2):
                load_outputs(0, slot, slot)
            sp.wait_ge(inverted, 3)
            sp.dma_start(inv_d.rearrange("h (a n) -> (h a) n", n=BANK), sums[:, 0, :]).then_inc(sums_in, 16)
            sp.wait_ge(sums_in, 64)
            run_steps(sp, step, CH, 2, first=2, tail=2)
            for i in range(2):
                sp.wait_ge(x1_stored[i], 16 * (CH // 2))

        @block.tensor
        def _(pe):
            def step(base, slot):
                if (c := at(base, slot, 1, 2, CH)) is not None:
                    par = (slot - 1) % 2
                    pe.wait_ge(ohi_done, KT * c + KT)
                    pe.wait_ge(olo_done, KT * c + KT)
                    for t in range(TT):
                        need(pe, x1_done, TT * (c - 2) + t + 1)
                        parts = [(a, b, kt) for kt in range(KT)
                                 for a, b in ((oT_hi, w_hi), (oT_hi, w_lo), (oT_lo, w_hi))]
                        for n, (a, b, kt) in enumerate(parts):
                            mm = pe.matmul(ps[:, 4 * par + t, :], a[par][:, kt, P * t:P * (t + 1)], b[:, kt, :],
                                           start=(n == 0), stop=(n == len(parts) - 1))
                        mm.then_inc(out_done, 1)

            pe.wait_ge(setup, 2)
            run_steps(pe, step, CH, 2, first=2, tail=1)

        @block.scalar
        def _(act):
            def step(base, slot):
                if (s := at(base, slot, 0, 2, CH)) is not None:
                    need(act, out_done, TT * (s - 1))
                    for kt in range(KT):
                        act.wait_ge(div_done, KT * s + kt + 1)
                        act.activation(oT_hi[slot][:, kt, :], oT_in[slot][:, kt, :], ACT.Identity).then_inc(ohi_done, 1)
                    for j in range(PER_STEP):
                        n = PER_STEP * s + j
                        layer, cols = piece(s, j)
                        wait_alone(act, weight_done, n + 1, passed)
                        act.activation(flat[layer][0][:, cols], weight[j % 2][:, :], ACT.Identity).then_inc(whi_done, 1)

            act.wait_ge(w_in, 48)
            act.activation(tanhs[:, :], gates[:, :], ACT.Tanh).then_inc(tanh_done, 1)
            run_steps(act, step, CH, 2, first=2)
            act.wait_ge(end, 2)
            act.activation(small[:, 1, :], small[:, 0, :], ACT.Sqrt, bias=eps[:, 0:1]).then_inc(root, 1)
            act.wait_ge(end, 5)
            act.activation(A["root2"][:, :], small[:, 4, :], ACT.Sqrt, bias=eps[:, 0:1]).then_inc(root, 1)

        @block.vector
        def _(dve):
            def split(s, j):
                layer, cols = piece(s, j)
                dve.wait_ge(whi_done, PER_STEP * s + j + 1)
                dve.tensor_tensor(flat[layer][1][:, cols], weight[j % 2][:, :], flat[layer][0][:, cols].bitcast(F32),
                                  ALU.subtract).then_inc(wlo_done, 1)

            def restore(s, j):
                layer, cols = piece(s, j)
                if j == 0 and layer == 0:
                    need(dve, w1_loaded, 32 * (s == 0))
                if j == 0 and layer == 1:
                    dve.wait_ge(w2_loaded, 32 * (s - CH // 2) + 32)
                need(dve, wlo_done, PER_STEP * s + j - 1)
                dve.scalar_tensor_tensor(weight[j % 2][:, :], codes[layer][:, cols], -ZERO_POINT, scales[layer][:, cols],
                                         ALU.add, ALU.mult) \
                    .then_inc(weight_done, 1)
                if j > 0:
                    split(s, j - 1)

            def step(base, slot):
                if (s := at(base, slot, 0, 2, CH)) is not None:
                    for kt in range(KT):
                        dve.wait_ge(ohi_done, KT * s + kt + 1)
                        dve.tensor_tensor(oT_lo[slot][:, kt, :], oT_in[slot][:, kt, :], oT_hi[slot][:, kt, :].bitcast(F32),
                                          ALU.subtract).then_inc(olo_done, 1)
                if (c := at(base, slot, 1, 2, CH)) is not None:
                    par = (slot - 1) % 2
                    dve.wait_ge(biased, c + 1)
                    for t in range(TT):
                        dve.wait_ge(out_done, TT * c + t + 1)
                        dve.scalar_tensor_tensor(x_in[par][:, t, :], ps[:, 4 * par + t, :], tanhs[:, 0:1],
                                                 x_in[par][:, t, :], ALU.mult, ALU.add).then_inc(x1_done, 1)
                s = at(base, slot, 0, 2, CH)
                if c is not None:
                    need(dve, mv_done, TT * c)
                for j in range(PER_STEP):
                    if s is not None:
                        restore(s, j)
                    if c is not None:
                        dve.wait_ge(x1_done, TT * c + j + 1)
                        dve.bn_stats(stats[:, j, :], x_in[par][:, j, :]).then_inc(stat_done, 1)
                if s is not None:
                    split(s, PER_STEP - 1)
                if c is not None:
                    need(dve, kept, c)
                    for t in range(TT):
                        wait_alone(dve, stat_done, TT * c + t + 1, passed)
                        dve.bn_aggr(meanvar[:, t, :], stats[:, t, :]).then_inc(mv_done, 1)
                    dve.wait_ge(mv_done, TT * c + TT)
                    dve.tensor_copy(mv_all[:, bass.ds(TT * c, TT), :], meanvar[:, :, :]).then_inc(kept, 1)

            dve.wait_ge(sums_in, 48)
            dve.tensor_tensor(sums[:, 0, :], sums[:, 0, :], sums[:, 1, :], ALU.add).then_inc(inverted, 1)
            dve.wait_ge(inverted, 1)
            dve.tensor_tensor(sums[:, 0, :], sums[:, 0, :], sums[:, 2, :], ALU.add).then_inc(inverted, 1)
            dve.wait_ge(inverted, 2)
            dve.reciprocal(sums[:, 0, :], sums[:, 0, :]).then_inc(inverted, 1)
            dve.wait_ge(x_loaded[1], 16)
            dve.tensor_copy(w_hi[:, :, :], w_stage[:, :, :]).then_inc(setup, 1)
            dve.wait_ge(setup, 1)
            dve.tensor_tensor(w_lo[:, :, :], w_stage[:, :, :], w_hi[:, :, :].bitcast(F32), ALU.subtract) \
                .then_inc(setup, 1)
            dve.wait_ge(tanh_done, 1)
            dve.wait_ge(w_in, 48)
            dve.tensor_scalar(bias[:, :], bias[:, :], tanhs[:, 0:1], None, ALU.mult).then_inc(setup, 1)
            run_steps(dve, step, CH, 2, first=2, tail=1)
            dve.memset(eps[:, :], EPS).then_inc(end, 1)
            dve.wait_ge(kept, CH)
            dve.wait_ge(wlo_done, 2 * PIECES)
            dve.tensor_copy(small[:, 0, :], mv_all[:, :, 1]).then_inc(end, 1)
            dve.tensor_copy(A["mean1"][:, :], mv_all[:, :, 0]).then_inc(end, 1)
            dve.wait_ge(root, 1)
            dve.reciprocal(small[:, 2, :], small[:, 1, :]).then_inc(end, 1)
            dve.wait_ge(end, 4)
            dve.tensor_tensor(small[:, 3, :], small[:, 0, :], small[:, 2, :], ALU.mult).then_inc(root, 1)
            dve.wait_ge(root, 2)
            dve.tensor_tensor(small[:, 4, :], small[:, 3, :], small[:, 2, :], ALU.mult).then_inc(end, 1)
            dve.wait_ge(root, 3)
            dve.reciprocal(small[:, 5, :], A["root2"][:, :]).then_inc(end, 1)
            dve.wait_ge(end, 6)
            dve.tensor_tensor(A["norm12"][:, :], small[:, 2, :], small[:, 5, :], ALU.mult).then_inc(end, 1)
            dve.tensor_scalar(A["keep2"][:, :], A["root2"][:, :], tanhs[:, 1:2], None, ALU.mult).then_inc(end, 1)
            dve.tensor_scalar(A["half_gate"][:, :], tanhs[:, 1:2], 0.5, None, ALU.mult).then_inc(end, 1)


def feed_forward(k, A, x1_d, w1, w2, gamma, beta, b1, b2, out):
    nc, ps = k.nc, k.ps
    R, _, C = x1_d.shape
    KT, TT = C // P, BANK // P
    F = w1[0].shape[2]
    FT = F // P
    CH = R // TT
    UNROLL = 2 * FT
    STEPS = CH * FT
    LAG = 2
    out_rows = out.rearrange("b (t p) c -> (b t) p c", p=P)

    with ExitStack() as ctx:
        sb = lambda name, shape, dt=F32: k.sb(ctx, "ff_" + name, shape, dt)
        sem = lambda name: k.sem(ctx, "ff_" + name)
        gam = sb("gam", [P, KT])
        bet = sb("bet", [P, KT])
        b1_t = sb("b1_t", [P, FT])
        b2_half = sb("b2_half", [P, C])
        x_in = [sb(f"x_in{i}", [P, TT, C]) for i in range(2)]
        coef = sb("coef", [P, 3, TT])
        normed = sb("normed", [P, TT, C])
        h = [sb(f"h{i}", [P, BANK]) for i in range(2)]
        h_hi = [sb(f"h_hi{i}", [P, KT, BANK], F32R) for i in range(2)]
        h_lo = [sb(f"h_lo{i}", [P, KT, BANK], F32R) for i in range(2)]
        y = [sb(f"y{i}", [P, BANK]) for i in range(2)]
        y_hi = [sb(f"y_hi{i}", [P, BANK], F32R) for i in range(2)]
        y_lo = [sb(f"y_lo{i}", [P, BANK], F32R) for i in range(2)]

        c_in = sem("c_in")
        setup = sem("setup")
        x_loaded = [sem(f"x_loaded{i}") for i in range(2)]
        coef_done = sem("coef_done")
        normed_done = sem("normed_done")
        kept_done = sem("kept_done")
        base_done = sem("base_done")
        h_turned = sem("h_turned")
        h_done = sem("h_done")
        hhi_done = sem("hhi_done")
        hlo_done = sem("hlo_done")
        first_done = sem("first_done")
        y_done = sem("y_done")
        yhi_done = sem("yhi_done")
        ylo_done = sem("ylo_done")
        second_done = sem("second_done")
        out_done = sem("out_done")
        out_stored = [sem(f"out_stored{i}") for i in range(2)]
        block = ctx.enter_context(nc.Block())

        COEFS, NORM, TURN = 5, 6, 10

        def next_chunk(base, slot):
            c = 2 * base + slot // FT + 1
            return None if isinstance(c, int) and c >= CH else c

        @block.sync
        def _(sp):
            def step(base, slot):
                c = 2 * base + slot
                sp.wait_ge(out_done, TT * c + TT)
                sp.dma_start(out_rows[bass.ds(TT * c, TT)].rearrange("t p c -> p t c"), x_in[slot][:, :, :]) \
                    .then_inc(out_stored[slot], 16)
                if not isinstance(c, int) or c + 2 < CH:
                    sp.wait_ge(out_stored[slot], 16 * base + 16)
                    load(slot, c + 2)

            def load(par, c):
                sp.dma_start(x_in[par][:, :, :], x1_d[bass.ds(TT * c, TT)].rearrange("t p c -> p t c")) \
                    .then_inc(x_loaded[par], 16)

            load(0, 0)
            for dst, src in ((gam, gamma), (bet, beta), (b1_t, b1)):
                sp.dma_start(dst[:, :], src.rearrange("(m p) -> p m", p=P),
                             allow_slow_non_contiguous=True).then_inc(c_in, 16)
            sp.dma_start(b2_half[:, :], b2.partition_broadcast(P)).then_inc(c_in, 16)
            load(1, 1)
            run_steps(sp, step, CH, 2, first=1, last=1)
            for i in range(2):
                sp.wait_ge(out_stored[i], 16 * (CH // 2))

        def turn(pe, c, kt):
            pe.wait_ge(normed_done, TT * c + TT)
            need(pe, h_done, KT * c + kt - 1)
            for t in range(TT):
                mm = pe.transpose(ps[:, 6 + kt % 2, P * t:P * (t + 1)], normed[:, t, P * kt:P * (kt + 1)],
                                  A["ident"][:, :])
            mm.then_inc(h_turned, 1)

        @block.tensor
        def _(pe):
            def step(base, slot):
                if (s := at(base, slot, 0, UNROLL, STEPS)) is not None:
                    f = slot % FT
                    if f == 0:
                        c = 2 * base + slot // FT
                        pe.wait_ge(hhi_done, KT * c + KT)
                        pe.wait_ge(hlo_done, KT * c + KT)
                    need(pe, y_done, s - 1)
                    hi, lo = h_hi[slot // FT], h_lo[slot // FT]
                    parts = [(a, b, kt) for kt in range(KT) for a, b in ((0, hi), (1, hi), (0, lo))]
                    for n, (a, b, kt) in enumerate(parts):
                        mm = pe.matmul(ps[:, 4 + f % 2, :], w1[a][:, kt, P * f:P * (f + 1)], b[:, kt, :],
                                       start=(n == 0), stop=(n == len(parts) - 1))
                    mm.then_inc(first_done, 1)
                    if TURN <= f < TURN + KT and (c := next_chunk(base, slot)) is not None:
                        turn(pe, c, f - TURN)
                if (e := at(base, slot, LAG, UNROLL, STEPS)) is not None:
                    f = (slot - LAG) % FT
                    chunk = 2 * base + (slot - LAG) // FT
                    pe.wait_ge(ylo_done, e + 1)
                    for t in range(TT):
                        if f == 0:
                            need(pe, out_done, TT * (chunk - 1) + t + 1)
                        cols = slice(P * t, P * (t + 1))
                        parts = ((y_hi, 0), (y_hi, 1), (y_lo, 0))
                        for n, (a, b) in enumerate(parts):
                            mm = pe.matmul(ps[:, t, :], a[f % 2][:, cols], w2[b][:, f, :],
                                           start=(f == 0 and n == 0), stop=(f == FT - 1 and n == 2))
                    mm.then_inc(second_done, 1)

            for kt in range(KT):
                turn(pe, 0, kt)
            run_steps(pe, step, STEPS, UNROLL, first=1, last=1, tail=LAG)

        def shape_h(act, c, kt):
            act.wait_ge(h_turned, KT * c + kt + 1)
            need(act, hlo_done, KT * c + kt - 1)
            act.activation(h[kt % 2][:, :], ps[:, 6 + kt % 2, :], ACT.Identity, bias=bet[:, kt:kt + 1],
                           scale=gam[:, kt:kt + 1]).then_inc(h_done, 1)

        @block.scalar
        def _(act):
            def step(base, slot):
                if (s := at(base, slot, 0, UNROLL, STEPS)) is not None:
                    f = slot % FT
                    act.wait_ge(first_done, s + 1)
                    need(act, ylo_done, s - 1)
                    act.activation(y[f % 2][:, :], ps[:, 4 + f % 2, :], ACT.Silu, bias=b1_t[:, f:f + 1]) \
                        .then_inc(y_done, 1)
                    if TURN <= f < TURN + KT and (c := next_chunk(base, slot)) is not None:
                        shape_h(act, c, f - TURN)

            act.wait_ge(c_in, 64)
            for kt in range(KT):
                shape_h(act, 0, kt)
            run_steps(act, step, STEPS, UNROLL, first=1, last=1)

        @block.gpsimd
        def _(pool):
            def step(base, slot):
                c = 2 * base + slot
                pool.wait_ge(kept_done, TT * c + TT)
                pool.tensor_tensor(x_in[slot][:, :, :], x_in[slot][:, :, :],
                                   b2_half[:, :].unsqueeze(1).to_broadcast([P, TT, C]), ALU.add).then_inc(base_done, 1)

            pool.wait_ge(setup, 1)
            run_steps(pool, step, CH, 2, first=1)

        @block.vector
        def _(dve):
            def coefs(par, loads, c):
                dve.wait_ge(x_loaded[par], 16 * loads)
                need(dve, normed_done, TT * c)
                need(dve, kept_done, TT * c)
                for i, src in enumerate(("mean1", "norm12", "keep2")):
                    dve.tensor_copy(coef[:, i, :], A[src][:, bass.ds(TT * c, TT)]).then_inc(coef_done, 1)

            def norm(par, c, t):
                dve.wait_ge(coef_done, 3 * c + 3)
                if t == 0:
                    need(dve, h_turned, KT * c)
                dve.tensor_scalar(normed[:, t, :], x_in[par][:, t, :], coef[:, 0, t:t + 1], coef[:, 1, t:t + 1],
                                  ALU.subtract, ALU.mult).then_inc(normed_done, 1)
                dve.wait_ge(normed_done, TT * c + t + 1)
                dve.scalar_tensor_tensor(x_in[par][:, t, :], normed[:, t, :], coef[:, 2, t:t + 1],
                                         x_in[par][:, t, :], ALU.mult, ALU.add).then_inc(kept_done, 1)

            def split_h(par, c, kt):
                need(dve, first_done, FT * (c - 1))
                dve.wait_ge(h_done, KT * c + kt + 1)
                dve.tensor_copy(h_hi[par][:, kt, :], h[kt % 2][:, :]).then_inc(hhi_done, 1)
                dve.wait_ge(hhi_done, KT * c + kt + 1)
                dve.tensor_tensor(h_lo[par][:, kt, :], h[kt % 2][:, :], h_hi[par][:, kt, :].bitcast(F32),
                                  ALU.subtract).then_inc(hlo_done, 1)

            def step(base, slot):
                if (s := at(base, slot, 0, UNROLL, STEPS)) is not None:
                    f = slot % FT
                    dve.wait_ge(y_done, s + 1)
                    need(dve, second_done, s - 1)
                    dve.tensor_copy(y_hi[f % 2][:, :], y[f % 2][:, :]).then_inc(yhi_done, 1)
                    dve.wait_ge(yhi_done, s + 1)
                    dve.tensor_tensor(y_lo[f % 2][:, :], y[f % 2][:, :], y_hi[f % 2][:, :].bitcast(F32),
                                      ALU.subtract).then_inc(ylo_done, 1)
                    c = next_chunk(base, slot)
                    if c is not None:
                        par, loads = (slot // FT + 1) % 2, base + 1 + (slot // FT)
                        if f == COEFS:
                            coefs(par, loads, c)
                        if NORM <= f < NORM + TT:
                            norm(par, c, f - NORM)
                        if TURN <= f < TURN + KT:
                            split_h(par, c, f - TURN)
                if (slot - LAG) % FT == FT - 1 and at(base, slot, LAG, UNROLL, STEPS) is not None:
                    chunk = 2 * base + (slot - LAG) // FT
                    par = (slot - LAG) // FT % 2
                    dve.wait_ge(second_done, FT * chunk + FT)
                    dve.wait_ge(base_done, chunk + 1)
                    for t in range(TT):
                        dve.scalar_tensor_tensor(x_in[par][:, t, :], ps[:, t, :], A["half_gate"][:, 0:1],
                                                 x_in[par][:, t, :], ALU.mult, ALU.add).then_inc(out_done, 1)

            dve.wait_ge(c_in, 64)
            dve.tensor_scalar(b2_half[:, :], b2_half[:, :], A["half_gate"][:, 0:1], None, ALU.mult).then_inc(setup, 1)
            coefs(0, 1, 0)
            for t in range(TT):
                norm(0, 0, t)
            for kt in range(KT):
                split_h(0, 0, kt)
            run_steps(dve, step, STEPS, UNROLL, first=1, last=1, tail=LAG)


def weight_space(k, ctx, name, tiles, cols):
    with ExitStack() as first:
        raw = [k.sb(first, f"{name}_scales", [P, tiles * cols]), k.sb(first, f"{name}_codes", [P, tiles, cols], I32)]
    return raw, [k.sb(ctx, f"{name}_{part}", [P, tiles, cols], F32R) for part in ("hi", "lo")]


def gated_cross_attention_block(nc, x, ctx_768, g_xattn, g_ffn, wq, bq, wk, bk, wv, bv, wo, bo,
                                ln_gamma, ln_beta, fc1_q, fc1_scales, fc1_bias, fc2_q, fc2_scales, fc2_bias, out):
    B, SQ, C = x.shape
    SK = ctx_768.shape[1]
    F = fc1_q.shape[1]
    ROWS = B * SQ // P

    def dram(name, shape):
        return nc.dram_tensor(name, shape, F32, kind="Internal").ap()

    qT_d = [dram(f"qT_{part}", (B * C, SQ)) for part in ("hi", "lo")]
    kT_d = [dram(f"kT_{part}", (B * C, SK)) for part in ("hi", "lo")]
    v_d = dram("v_heads", (B * HEADS, P, SK // P * D))
    oT_d = dram("oT", (B * C, SQ))
    sum_d = [dram(f"sums{i}", (B * HEADS, SQ)) for i in range(3)]
    inv_d = dram("inverse_sums", (B * HEADS, SQ))
    x1_d = dram("x1", (ROWS, P, C))

    with ExitStack() as ctx:
        k = Core(nc, ctx)
        A = {name: k.sb(ctx, name, shape, dt) for name, shape, dt in (
            ("ident", [P, P], F32), ("fold", [P, D], F32), ("clip_path", [1, 1], I32), ("clip_high", [P, 1], F32),
            ("clip_low", [P, 1], F32), ("mean1", [P, ROWS], F32), ("root2", [P, ROWS], F32),
            ("norm12", [P, ROWS], F32), ("keep2", [P, ROWS], F32), ("half_gate", [P, 1], F32))}
        with ExitStack() as bounds:
            A |= {name: k.sb(bounds, name, [P, BANK]) for name in ("q_sq_sum", "k_sq_sum", "not_finite")}
            project_queries(k, A, x, wq, bq, qT_d)
            project_keys_values(k, A, ctx_768, wk, bk, wv, bv, kT_d, v_d)
        w1_raw, w1 = weight_space(k, ctx, "w1", C // P, F)
        w1_loaded = k.sem(ctx, "w1_loaded")
        attend(k, A, (B, SQ, SK), qT_d, kT_d, v_d, oT_d, sum_d, w1_raw, fc1_q, fc1_scales, w1_loaded)
        w2_raw, w2 = weight_space(k, ctx, "w2", F // P, C)
        project_out(k, A, x, oT_d, sum_d, inv_d, wo, bo, g_xattn, g_ffn, x1_d, (w1_raw, w2_raw), (w1, w2),
                    fc2_q, fc2_scales, w1_loaded)
        feed_forward(k, A, x1_d, w1, w2, ln_gamma, ln_beta, fc1_bias, fc2_bias, out)


_INS = ['x', 'ctx_768', 'g_xattn', 'g_ffn', 'L0_xattn_Wq', 'L0_xattn_bq', 'L0_xattn_Wk', 'L0_xattn_bk',
        'L0_xattn_Wv', 'L0_xattn_bv', 'L0_xattn_Wo', 'L0_xattn_bo', 'L0_ffn_ln_gamma', 'L0_ffn_ln_beta',
        'L0_ffn_fc1_q', 'L0_ffn_fc1_scales', 'L0_ffn_fc1_bias', 'L0_ffn_fc2_q', 'L0_ffn_fc2_scales',
        'L0_ffn_fc2_bias']
_OUTS = [((4, 1024, 512), 'float32')]


def kernel(**inputs):
    import numpy as _np
    import concourse.bacc as _bacc
    from concourse import mybir as _mybir
    from concourse.bass_utils import run_bass_kernel_spmd as _run

    nc = _bacc.Bacc("TRN2", target_bir_lowering=False, num_devices=1)
    arrays, args = {}, []
    for name in _INS:
        a = _np.ascontiguousarray(inputs[name])
        arrays[f"in_{name}_dram"] = a
        args.append(nc.dram_tensor(f"in_{name}_dram", a.shape, _mybir.dt.from_np(a.dtype), kind="ExternalInput").ap())
    for i, (shape, dtype) in enumerate(_OUTS):
        dt = _mybir.dt.from_np(_np.dtype(dtype))
        args.append(nc.dram_tensor(f"out_{i}_dram", shape, dt, kind="ExternalOutput").ap())
    gated_cross_attention_block(nc, *args)
    r = _run(nc, [arrays], core_ids=[0])
    got = tuple(r.results[0][f"out_{i}_dram"] for i in range(len(_OUTS)))
    return got[0]
```
